# Optimizing a Trainium2 kernel written in Bass

```python
import numpy as np
import jax
import jax.numpy as jnp

def _softmax(x, axis=-1):
    return jax.nn.softmax(x, axis=axis)

def _gelu(x):
    return jax.nn.gelu(x, approximate=True)

def _silu(x):
    return jax.nn.silu(x)

def _sigmoid(x):
    return jax.nn.sigmoid(x)

def _layernorm(x, axis=-1, eps=1e-05):
    m = jnp.mean(x, axis=axis, keepdims=True)
    v = jnp.var(x, axis=axis, keepdims=True)
    return (x - m) / jnp.sqrt(v + eps)

def _scatter_add(tgt, idx, src, axis=0):
    return tgt.at[idx].add(src)

def _segment_sum(src, seg, n):
    return jax.ops.segment_sum(src, seg, n)
kernel_name = 'mk_adaln_attn_ffn_d1_seqx_r8_f1234f'

def setup_inputs(seed: int=0):
    np.random.seed(seed)
    _w = jnp.asarray

    def _rec_inputs():
        import jax
        import jax.numpy as jnp
        _rk = jax.random.key(seed)
        x = -0.000125 + 0.9999 * jax.random.normal(jax.random.fold_in(_rk, 1), (32, 32, 512), jnp.float32)
        _lenS = 32 - jax.random.randint(jax.random.fold_in(_rk, 7), (32,), 0, max(1, 32 // 4) + 1, jnp.int32)
        _lenS2 = 32 - jax.random.randint(jax.random.fold_in(_rk, 8), (32,), 0, max(1, 32 // 4) + 1, jnp.int32)
        itok_B_0_23 = jax.random.randint(jax.random.fold_in(_rk, 11), (32,), 0, 24, jnp.int32)
        itok_B_0_2 = jax.random.randint(jax.random.fold_in(_rk, 12), (32,), 0, 3, jnp.int32)
        return (x, itok_B_0_23, itok_B_0_2)
    x, itok_B_0_23, itok_B_0_2 = _rec_inputs()

    def _L0_cond_setup():
        import jax, jax.numpy as jnp
        import numpy as np
        R = 16
        ALPHA = 32
        SCALING = ALPHA / R
        SLOTS = 32
        IN_F = 512
        OUT_F = 512
        B, T = (8, 128)
        key = jax.random.key(seed)
        k1, k2, k3, k4, k5, k6 = jax.random.split(key, 6)
        x = jax.random.normal(k1, (B, T, IN_F), dtype=jnp.float32)
        adapter_mapping = jax.random.randint(k2, (B,), 0, SLOTS, dtype=jnp.int32)
        W = jax.random.normal(k3, (OUT_F, IN_F), dtype=jnp.float32) * 0.02
        b = jax.random.normal(k4, (OUT_F,), dtype=jnp.float32) * 0.02
        lora_As = jax.random.normal(k5, (SLOTS, IN_F, R), dtype=jnp.float32) * 0.02
        lora_Bs = jax.random.normal(k6, (SLOTS, R, OUT_F), dtype=jnp.float32) * 0.02
        return {'x': x, 'adapter_mapping': adapter_mapping, 'W': W, 'b': b, 'lora_As': lora_As, 'lora_Bs': lora_Bs}
    _L0_cond_all = _L0_cond_setup()
    _L0_cond_in = {k: v for k, v in _L0_cond_all.items() if k in ('W', 'b', 'lora_As', 'lora_Bs')}
    del _L0_cond_all

    def _L0_attn_setup():
        import jax, jax.numpy as jnp
        import numpy as np
        D_IN = 512
        D_OUT = 512
        HEADS = 32
        KV_GROUPS = 8
        HEAD_DIM = D_OUT // HEADS
        GROUP_SIZE = HEADS // KV_GROUPS
        CONTEXT_LEN = 512
        ROPE_BASE = 10000.0
        BATCH, TOKENS = (1, 256)

        def _rope_tables(context_length, head_dim, theta_base):
            inv_freq = 1.0 / theta_base ** (np.arange(0, head_dim, 2)[:head_dim // 2].astype(np.float32) / head_dim)
            pos = np.arange(context_length, dtype=np.float32)
            angles = pos[:, None] * inv_freq[None, :]
            angles = np.concatenate([angles, angles], axis=1)
            return (jnp.asarray(np.cos(angles), jnp.float32), jnp.asarray(np.sin(angles), jnp.float32))

        def _apply_rope(x, cos, sin):
            hd = x.shape[-1]
            x1, x2 = (x[..., :hd // 2], x[..., hd // 2:])
            rotated = jnp.concatenate([-x2, x1], axis=-1)
            return x * cos + rotated * sin
        key = jax.random.key(seed)
        kx, kq, kk, kv, ko = jax.random.split(key, 5)
        s = 0.02
        x = jax.random.normal(kx, (BATCH, TOKENS, D_IN), jnp.float32)
        Wq = jax.random.normal(kq, (D_IN, D_OUT), jnp.float32) * s
        Wk = jax.random.normal(kk, (D_IN, KV_GROUPS * HEAD_DIM), jnp.float32) * s
        Wv = jax.random.normal(kv, (D_IN, KV_GROUPS * HEAD_DIM), jnp.float32) * s
        Wo = jax.random.normal(ko, (D_OUT, D_OUT), jnp.float32) * s
        cos, sin = _rope_tables(CONTEXT_LEN, HEAD_DIM, ROPE_BASE)
        return {'x': x, 'Wq': Wq, 'Wk': Wk, 'Wv': Wv, 'Wo': Wo, 'cos': cos, 'sin': sin}
    _L0_attn_all = _L0_attn_setup()
    _L0_attn_in = {k: v for k, v in _L0_attn_all.items() if k in ('Wq', 'Wk', 'Wv', 'Wo', 'cos', 'sin')}
    del _L0_attn_all

    def _L0_cond2_setup():
        import jax, jax.numpy as jnp
        import numpy as np
        B, S, D_IN, D_OUT = (4, 256, 512, 512)
        R, NUM_LABELERS = (32, 5)
        LORA_SCALING = 16 / 32
        key = jax.random.key(seed)
        k1, k2, k3, k4, k5 = jax.random.split(key, 5)
        x = jax.random.normal(k1, (B, S, D_IN), dtype=jnp.float32)
        labeler_index = jax.random.randint(k2, (B,), 0, NUM_LABELERS, dtype=jnp.int64)
        W = jax.random.normal(k3, (D_OUT, D_IN), dtype=jnp.float32) * 0.02
        lora_A = jax.random.normal(k4, (NUM_LABELERS, D_IN, R), dtype=jnp.float32) * 0.02
        lora_B_w = jax.random.normal(k5, (D_OUT, R), dtype=jnp.float32) * 0.02
        return {'x': x, 'labeler_index': labeler_index, 'W': W, 'lora_A': lora_A, 'lora_B_w': lora_B_w}
    _L0_cond2_all = _L0_cond2_setup()
    _L0_cond2_in = {k: v for k, v in _L0_cond2_all.items() if k in ('W', 'lora_A', 'lora_B_w')}
    del _L0_cond2_all

    def _L0_ffn_setup():
        import jax, jax.numpy as jnp
        import numpy as np
        LORA_SCALE = 16.0 / jnp.sqrt(16.0)
        TOP_K = 2
        key = jax.random.key(seed)
        k1, k2, k3, k4 = jax.random.split(key, 4)
        B_, S, D, O, E, R = (4, 256, 512, 512, 4, 16)
        x = jax.random.normal(k1, (B_, S, D), dtype=jnp.float32)
        router_w = jax.random.normal(k2, (E, D), dtype=jnp.float32) * 0.02
        A = jax.random.normal(k3, (E, R, D), dtype=jnp.float32) * 0.02
        B = jax.random.normal(k4, (O,), dtype=jnp.float32)
        B = jax.random.normal(k4, (E, O, R), dtype=jnp.float32) * 0.02
        return {'x': x, 'router_w': router_w, 'A': A, 'B': B}
    _L0_ffn_all = _L0_ffn_setup()
    _L0_ffn_in = {k: v for k, v in _L0_ffn_all.items() if k in ('router_w', 'A', 'B')}
    del _L0_ffn_all
    return {'x': x, 'itok_B_0_23': itok_B_0_23, 'itok_B_0_2': itok_B_0_2, 'L0_cond_W': _L0_cond_in['W'], 'L0_cond_b': _L0_cond_in['b'], 'L0_cond_lora_As': _L0_cond_in['lora_As'], 'L0_cond_lora_Bs': _L0_cond_in['lora_Bs'], 'L0_attn_Wq': _L0_attn_in['Wq'], 'L0_attn_Wk': _L0_attn_in['Wk'], 'L0_attn_Wv': _L0_attn_in['Wv'], 'L0_attn_Wo': _L0_attn_in['Wo'], 'L0_attn_cos': _L0_attn_in['cos'], 'L0_attn_sin': _L0_attn_in['sin'], 'L0_cond2_W': _L0_cond2_in['W'], 'L0_cond2_lora_A': _L0_cond2_in['lora_A'], 'L0_cond2_lora_B_w': _L0_cond2_in['lora_B_w'], 'L0_ffn_router_w': _L0_ffn_in['router_w'], 'L0_ffn_A': _L0_ffn_in['A'], 'L0_ffn_B': _L0_ffn_in['B']}

def reference(x, itok_B_0_23, itok_B_0_2, L0_cond_W, L0_cond_b, L0_cond_lora_As, L0_cond_lora_Bs, L0_attn_Wq, L0_attn_Wk, L0_attn_Wv, L0_attn_Wo, L0_attn_cos, L0_attn_sin, L0_cond2_W, L0_cond2_lora_A, L0_cond2_lora_B_w, L0_ffn_router_w, L0_ffn_A, L0_ffn_B):
    import jax
    import jax.numpy as jnp

    def _L0_cond_ref(x, adapter_mapping, W, b, lora_As, lora_Bs):
        import jax, jax.numpy as jnp
        import numpy as np
        R = 16
        ALPHA = 32
        SCALING = ALPHA / R
        SLOTS = 32
        IN_F = 512
        OUT_F = 512
        B, T = (8, 128)
        base_out = jnp.einsum('bti,oi->bto', x, W) + b
        A = lora_As[adapter_mapping]
        Bm = lora_Bs[adapter_mapping]
        lora_h = jnp.einsum('bti,bir->btr', x, A)
        lora_out = jnp.einsum('btr,bro->bto', lora_h, Bm)
        return base_out + lora_out * SCALING

    def _L0_attn_ref(x, Wq, Wk, Wv, Wo, cos, sin):
        import jax, jax.numpy as jnp
        import numpy as np
        D_IN = 512
        D_OUT = 512
        HEADS = 32
        KV_GROUPS = 8
        HEAD_DIM = D_OUT // HEADS
        GROUP_SIZE = HEADS // KV_GROUPS
        CONTEXT_LEN = 512
        ROPE_BASE = 10000.0
        BATCH, TOKENS = (1, 256)

        def _rope_tables(context_length, head_dim, theta_base):
            inv_freq = 1.0 / theta_base ** (np.arange(0, head_dim, 2)[:head_dim // 2].astype(np.float32) / head_dim)
            pos = np.arange(context_length, dtype=np.float32)
            angles = pos[:, None] * inv_freq[None, :]
            angles = np.concatenate([angles, angles], axis=1)
            return (jnp.asarray(np.cos(angles), jnp.float32), jnp.asarray(np.sin(angles), jnp.float32))

        def _apply_rope(x, cos, sin):
            hd = x.shape[-1]
            x1, x2 = (x[..., :hd // 2], x[..., hd // 2:])
            rotated = jnp.concatenate([-x2, x1], axis=-1)
            return x * cos + rotated * sin
        B, T, _ = x.shape
        q = (x @ Wq).reshape(B, T, HEADS, HEAD_DIM).transpose(0, 2, 1, 3)
        k = (x @ Wk).reshape(B, T, KV_GROUPS, HEAD_DIM).transpose(0, 2, 1, 3)
        v = (x @ Wv).reshape(B, T, KV_GROUPS, HEAD_DIM).transpose(0, 2, 1, 3)
        cos_t, sin_t = (cos[:T], sin[:T])
        q = _apply_rope(q, cos_t, sin_t)
        k = _apply_rope(k, cos_t, sin_t)
        qg = q.reshape(B, KV_GROUPS, GROUP_SIZE, T, HEAD_DIM)
        scores = jnp.einsum('bgptd,bgsd->bgpts', qg, k)
        causal = jnp.triu(jnp.ones((T, T), bool), k=1)
        scores = jnp.where(causal, -jnp.inf, scores)
        weights = jax.nn.softmax(scores / jnp.sqrt(jnp.float32(HEAD_DIM)), axis=-1)
        ctx = jnp.einsum('bgpts,bgsd->bgptd', weights, v)
        ctx = ctx.reshape(B, HEADS, T, HEAD_DIM).transpose(0, 2, 1, 3).reshape(B, T, D_OUT)
        return ctx @ Wo

    def _L0_cond2_ref(x, labeler_index, W, lora_A, lora_B_w):
        import jax, jax.numpy as jnp
        import numpy as np
        B, S, D_IN, D_OUT = (4, 256, 512, 512)
        R, NUM_LABELERS = (32, 5)
        LORA_SCALING = 16 / 32
        base = jnp.einsum('bsi,oi->bso', x, W)
        labelers_A = lora_A[labeler_index]
        low = jnp.einsum('bsi,bir->bsr', x, labelers_A)
        delta = jnp.einsum('bsr,or->bso', low, lora_B_w) * LORA_SCALING
        return base + delta

    def _L0_ffn_ref(x, router_w, A, B):
        import jax, jax.numpy as jnp
        import numpy as np
        LORA_SCALE = 16.0 / jnp.sqrt(16.0)
        TOP_K = 2
        D = x.shape[-1]
        flat = x.reshape(-1, D)
        logits = flat @ router_w.T
        topk_vals, topk_idx = jax.lax.top_k(logits, TOP_K)
        sparse = jnp.full_like(logits, -jnp.inf)
        rows = jnp.arange(logits.shape[0])[:, None]
        sparse = sparse.at[rows, topk_idx].set(topk_vals)
        gates = jax.nn.softmax(sparse, axis=-1)
        mid = jnp.einsum('tf,erf->ter', flat, A)
        all_deltas = jnp.einsum('ter,eor->teo', mid, B) * LORA_SCALE
        delta = jnp.einsum('te,teo->to', gates, all_deltas)
        return delta.reshape(*x.shape[:-1], -1)
    x = x + _L0_attn_ref(_L0_cond_ref(x, itok_B_0_23, L0_cond_W, L0_cond_b, L0_cond_lora_As, L0_cond_lora_Bs), L0_attn_Wq, L0_attn_Wk, L0_attn_Wv, L0_attn_Wo, L0_attn_cos, L0_attn_sin)
    x = x + _L0_ffn_ref(_L0_cond2_ref(x, itok_B_0_2, L0_cond2_W, L0_cond2_lora_A, L0_cond2_lora_B_w), L0_ffn_router_w, L0_ffn_A, L0_ffn_B)
    return x

_drawn_inputs = setup_inputs


def setup_inputs(seed=0):
    import zlib

    import numpy as np

    out = dict(_drawn_inputs(seed))
    spreads = {}
    factors = {'L0_cond_b': 8.0,
     'L0_cond_lora_As': 8.0,
     'L0_cond_lora_Bs': 8.0,
     'L0_attn_Wq': 8.0,
     'L0_attn_Wk': 8.0,
     'L0_attn_cos': 8.0,
     'L0_attn_sin': 8.0,
     'L0_cond2_lora_A': 7.624,
     'L0_cond2_lora_B_w': 7.707}
    for name, (base, spread) in spreads.items():
        noise = np.random.default_rng([zlib.crc32(name.encode()), seed]).standard_normal(out[name].shape)
        drawn = base * np.exp(spread * noise) if base else spread * noise
        out[name] = jnp.asarray(drawn.astype(out[name].dtype))
    for name, factor in factors.items():
        out[name] = (out[name] * factor).astype(out[name].dtype)
    return out
```

```python
from contextlib import ExitStack

import numpy as np
import concourse.bass as bass
from concourse import mybir

F32 = mybir.dt.float32
I32 = mybir.dt.int32
ALU = mybir.AluOpType
ACT = mybir.ActivationFunctionType
AX = mybir.AxisListType

P = 128
B, T, D = 32, 32, 512
KT = D // P
G = 4
SEQ = B // G
TOK = SEQ * T
TT = TOK // P
HD, NG, PH = 16, 8, 4
R1, R2 = 16, 32
SLOTS, LABELS = 32, 5
E, R = 4, 16
EW = E * R + E
PAIRS = SEQ // 2
NEG = -3.0e38

C_ID, C_ROT, C_CAUSAL, C_KG, C_SLOT, C_LABEL, C_VG, C_TRI, C_N = 0, 128, 256, 288, 296, 304, 308, 324, 340


def shape_constants():
    c = np.zeros((P, C_N), np.float32)
    p = np.arange(P)
    c[:, C_ID:C_ID + P] = np.eye(P)
    for m in range(P):
        if m % HD < HD // 2:
            c[m + HD // 2, C_ROT + m] = -1
        else:
            c[m - HD // 2, C_ROT + m] = 1
    c[:, C_CAUSAL:C_CAUSAL + T] = np.where(np.arange(T)[None] <= (p % T)[:, None], 0, NEG)
    c[:, C_KG:C_KG + NG] = (p // HD)[:, None] == np.arange(NG)
    c[:, C_SLOT:C_SLOT + SEQ] = 2.0 * ((p // R1)[:, None] == np.arange(SEQ))
    c[:, C_LABEL:C_LABEL + 4] = 0.5 * ((p // R2)[:, None] == np.arange(4))
    for half in range(2):
        c[:, C_VG + NG * half:C_VG + NG * (half + 1)] = (p // T + 4 * half)[:, None] == np.arange(NG)
    c[:, C_TRI:C_TRI + E * E] = (np.arange(E)[None, :] < np.arange(E)[:, None]).reshape(-1)
    return c


def program(nc, x, slot_ids, label_ids, cW, cb, lA, lB, wq, wk, wv, wo, cos, sin, w2, a2, bw, rw, fA, fB, consts, out):
    ctx = ExitStack()
    with ctx:
        def sb(name, shape, dt=F32):
            return ctx.enter_context(nc.sbuf_tensor(name, shape, dt))

        def sem(name):
            return ctx.enter_context(nc.semaphore(name))

        K = sb("K", [P, C_N])
        ids = sb("ids", [1, 2, B], I32)
        Wn = sb("Wn", [P, KT, D])
        WT = sb("WT", [P, KT, D])
        bias = sb("bias", [P, KT])
        Wqn = sb("Wqn", [P, KT, D])
        Wq = sb("Wq", [P, KT, PH, P])
        Wk = sb("Wk", [P, KT, P])
        Wv = sb("Wv", [P, KT, P])
        Wo = sb("Wo", [P, PH, D])
        W2 = sb("W2", [P, KT, D])
        Bw = sb("Bw", [P, KT, R2])
        Bw4 = sb("Bw4", [P, KT, 4, R2])
        RA = sb("RA", [EW, D])
        RAT = sb("RAT", [P, KT, EW])
        RT = sb("RT", [P, KT, EW])
        C4 = sb("C4", [P, EW])
        Bf = sb("Bf", [P, E, KT, R])
        Bk = sb("Bk", [P, KT, E, R])
        BT = sb("BT", [E * R, D])
        cs = sb("cs", [T, 2, HD])
        cs8 = sb("cs8", [T, 2, NG, HD])
        spread = sb("spread", [P, 4, 4, T])
        CS = sb("CS", [P, 2, T])
        xin = sb("xin", [P, TT, D])
        A1n = sb("A1n", [P, SEQ, KT, R1])
        A1 = sb("A1", [P, KT, SEQ, R1])
        B1 = sb("B1", [P, D])
        xT = sb("xT", [P, KT, TOK])
        hT = sb("hT", [P, TOK])
        yT = sb("yT", [P, KT, TOK])
        qk = sb("qk", [P, PH + 1, TOK])
        qkc = sb("qkc", [P, PH + 1, TOK])
        qks = sb("qks", [P, PH + 1, TOK])
        qr = sb("qr", [P, SEQ, PH, T])
        kr = sb("kr", [P, TOK])
        Kbd = sb("Kbd", [P, SEQ, NG, T])
        v = sb("v", [P, TT, P])
        Vbd = sb("Vbd", [P, 2, SEQ, P])
        sm = sb("sm", [P, PAIRS, 2 * NG, T])
        mx = sb("mx", [P, PAIRS, 2 * NG])
        ex = sb("ex", [P, PAIRS, 2 * NG, T])
        su = sb("su", [P, PAIRS, 2 * NG])
        ri = sb("ri", [P, PAIRS, 2 * NG])
        pr = sb("pr", [P, PAIRS, 2, 2, P])
        PT = sb("PT", [P, PAIRS, 2, 2, P])
        cT = sb("cT", [P, PH, SEQ, T])
        xres = sb("xres", [P, TT, D])
        x1 = sb("x1", [P, TT, D])
        x1T = sb("x1T", [P, TT, KT, P])
        A2n = sb("A2n", [P, SEQ, KT, R2])
        A2 = sb("A2", [P, KT, SEQ, R2])
        lT = sb("lT", [P, TT, P])
        mid = sb("mid", [P, TT, EW])
        m1 = sb("m1", [P, TT])
        lm = sb("lm", [P, TT, E])
        gt = sb("gt", [P, TT, E, E])
        eq = sb("eq", [P, TT, E, E])
        rk = sb("rk", [P, TT, E])
        le = sb("le", [P, TT, E])
        gw = sb("gw", [P, TT, E])
        gs = sb("gs", [P, TT])
        gr = sb("gr", [P, TT])
        gate = sb("gate", [P, TT, E])
        mg = sb("mg", [P, TT, P])
        mgT = sb("mgT", [E * R, TT, P])
        fin = sb("fin", [P, TT, D])

        bank = [ctx.enter_context(nc.psum_tensor(f"bank{i}", [P, 512], F32)) for i in range(8)]
        FR, SMALL, SC, PTB, CTX, OUT = bank[0:2], bank[2], bank[3:5], bank[5], bank[6], bank[7]
        TB = [OUT, PTB]

        d_ids, d_K, d_cs, d_W, d_b, d_q, d_k, d_v, d_o, d_w2, d_bw, d_ra, d_bf = map(
            sem, "d_ids d_K d_cs d_W d_b d_q d_k d_v d_o d_w2 d_bw d_ra d_bf".split())
        d_x, d_slot, d_xres, d_a2, d_out = map(sem, "d_x d_slot d_xres d_a2 d_out".split())
        w_ps, w_sb = sem("w_ps"), sem("w_sb")
        cs_laid, spread_laid, wq_laid, bw_laid, bf_laid, a1_laid, a2_laid = map(
            sem, "cs_laid spread_laid wq_laid bw_laid bf_laid a1_laid a2_laid".split())
        xT_ps, xT_sb, h_ps, h_sb, y_ps, y_sb, q_ps, q_sb, kv_ps, kv_sb = map(
            sem, "xT_ps xT_sb h_ps h_sb y_ps y_sb q_ps q_sb kv_ps kv_sb".split())
        rotk_ps, rotq_ps, k_sin, q_sin, k_cos, q_cos, k_rope, q_rope, kbd_sb, vr_ps, vbd_sb = map(
            sem, "rotk_ps rotq_ps k_sin q_sin k_cos q_cos k_rope q_rope kbd_sb vr_ps vbd_sb".split())
        sc_ps, masked, maxed, shifted, exped, summed, recip, normed, pt_ps, pt_sb, ctx_ps, ctx_sb = map(
            sem, "sc_ps masked maxed shifted exped summed recip normed pt_ps pt_sb ctx_ps ctx_sb".split())
        wo_ps, x1_sb, x1T_ps, x1T_sb, low_ps, low_sb, mid_ps, mid_sb = map(
            sem, "wo_ps x1_sb x1T_ps x1T_sb low_ps low_sb mid_ps mid_sb".split())
        g_step, g_exp, g_mid, mgT_ps, mgT_sb, dl_ps, fin_sb = map(
            sem, "g_step g_exp g_mid mgT_ps mgT_sb dl_ps fin_sb".split())

        ident = K[:, C_ID:C_ID + P]
        rot = K[:, C_ROT:C_ROT + P]
        xg = x.rearrange("(g t p) s d -> g p t (s d)", g=G, p=4) if False else x

        block = ctx.enter_context(nc.Block())

        @block.sync
        def _(sp):
            xf = x.rearrange("(g t s) u d -> g t (s u) d", g=G, t=TT)
            of = out.rearrange("(g t s) u d -> g t (s u) d", g=G, t=TT)

            def load_x(g):
                for t in range(TT):
                    sp.dma_start(xin[:, t, :], xf[bass.ds(g, 1), t].rearrange("a p d -> p (a d)")).then_inc(d_x, 16)

            def load_slots(g):
                for s in range(SEQ):
                    slot = sp.value_load(ids[0:1, 0, bass.ds(g * SEQ + s, 1)], min_val=0, max_val=SLOTS - 1)
                    sp.dma_start(A1n[:, s].rearrange("p k r -> p (k r)"),
                                 lA[bass.ds(slot, 1)].rearrange("a (p k) r -> p (a k r)", k=KT)).then_inc(d_slot, 16)
                    sp.dma_start(B1[R1 * s:R1 * (s + 1), :],
                                 lB[bass.ds(slot, 1)].rearrange("a r o -> (a r) o")).then_inc(d_slot, 16)

            def load_labels(g):
                for s in range(SEQ):
                    label = sp.value_load(ids[0:1, 1, bass.ds(g * SEQ + s, 1)], min_val=0, max_val=LABELS - 1)
                    sp.dma_start(A2n[:, s].rearrange("p k r -> p (k r)"),
                                 a2[bass.ds(label, 1)].rearrange("a (p k) r -> p (a k r)", k=KT)).then_inc(d_a2, 16)

            def load_xres(g):
                for t in range(TT):
                    sp.dma_start(xres[:, t, :], xf[bass.ds(g, 1), t].rearrange("a p d -> p (a d)")).then_inc(d_xres, 16)

            def front_loads(g):
                sp.wait_ge(xT_ps, 2 * g)
                load_x(g)
                sp.wait_ge(a1_laid, g)
                sp.wait_ge(y_ps, 2 * g)
                load_slots(g)

            def back_loads(g):
                sp.wait_ge(x1_sb, TT * g)
                load_xres(g)
                sp.wait_ge(a2_laid, g)
                load_labels(g)

            def store(g):
                for t in range(TT):
                    sp.wait_ge(fin_sb, TT * g + t + 1)
                    sp.dma_start(of[bass.ds(g, 1), t].rearrange("a p d -> p (a d)"), fin[:, t, :]).then_inc(d_out, 16)

            sp.dma_start(ids[:, 0], slot_ids.rearrange("(a b) -> a b", a=1)).then_inc(d_ids, 16)
            sp.dma_start(ids[:, 1], label_ids.rearrange("(a b) -> a b", a=1)).then_inc(d_ids, 16)
            sp.dma_start(K[:], consts).then_inc(d_K, 16)
            load_x(0)
            sp.dma_start(Wn[:], cW.rearrange("(c p) i -> p c i", p=P)).then_inc(d_W, 16)
            sp.wait_ge(d_ids, 32)
            load_slots(0)
            sp.dma_start(Wqn[:], wq.rearrange("(c p) n -> p c n", p=P)).then_inc(d_q, 16)
            sp.dma_start(Wk[:], wk.rearrange("(c p) n -> p c n", p=P)).then_inc(d_k, 16)
            sp.dma_start(Wv[:], wv.rearrange("(c p) n -> p c n", p=P)).then_inc(d_v, 16)
            front_loads(1)
            load_xres(0)
            load_labels(0)
            with sp.Fori(0, G - 2) as g:
                front_loads(g + 2)
                back_loads(g + 1)
                store(g)
            back_loads(G - 1)
            store(G - 2)
            store(G - 1)
            sp.wait_ge(d_out, 16 * TT * G)

        @block.scalar
        def _(act):
            act.dma_start(bias[:], cb.rearrange("(c p) -> p c", p=P), allow_slow_non_contiguous=True).then_inc(d_b, 16)
            act.dma_start(cs[:, 0], cos[0:T, :]).then_inc(d_cs, 16)
            act.dma_start(cs[:, 1], sin[0:T, :]).then_inc(d_cs, 16)
            act.dma_start(RA[0:E * R], fA.rearrange("e r d -> (e r) d")).then_inc(d_ra, 16)
            act.dma_start(RA[E * R:EW], rw).then_inc(d_ra, 16)
            act.dma_start(Bw[:], bw.rearrange("(c p) r -> p c r", p=P)).then_inc(d_bw, 16)
            act.dma_start(Bf[:].rearrange("p e k r -> p e (k r)"),
                          fB.rearrange("e (p k) r -> p e (k r)", k=KT)).then_inc(d_bf, 16)

            def copy(dst, src):
                return nc.scalar.copy(dst, src)

            def lay_adapters(g):
                act.wait_ge(d_slot, 16 * 2 * SEQ * (g + 1))
                if not (isinstance(g, int) and g == 0):
                    act.wait_ge(h_ps, g)
                copy(A1[:].rearrange("p k s r -> p s k r"), A1n[:]).then_inc(a1_laid, 1)

            def lay_labels(g):
                act.wait_ge(d_a2, 16 * SEQ * (g + 1))
                if not (isinstance(g, int) and g == 0):
                    act.wait_ge(low_ps, TT * g)
                copy(A2[:].rearrange("p k s r -> p s k r"), A2n[:]).then_inc(a2_laid, 1)

            def x_cols(g):
                for h in range(2):
                    act.wait_ge(xT_ps, 2 * g + h + 1)
                    copy(xT[:, 2 * h:2 * h + 2].rearrange("p k t -> p (k t)"), FR[h][:]).then_inc(xT_sb, 1)

            def y_cols(g, h):
                act.wait_ge(y_ps, 2 * g + h + 1)
                for c in (2 * h, 2 * h + 1):
                    nc.scalar.activation(yT[:, c, :], FR[h][:, (c % 2) * TOK:(c % 2 + 1) * TOK], ACT.Identity,
                                         bias=bias[:, c:c + 1]).then_inc(y_sb, 1)

            def q_cols(g, h):
                act.wait_ge(q_ps, 2 * g + h + 1)
                copy(qk[:, 2 * h:2 * h + 2].rearrange("p k t -> p (k t)"), FR[h][:]).then_inc(q_sb, 1)

            def kv_cols(g):
                act.wait_ge(kv_ps, g + 1)
                copy(qk[:, PH, :], SMALL[:, 0:TOK]).then_inc(kv_sb, 1)
                copy(v[:].rearrange("p t n -> p (t n)"), SMALL[:, TOK:2 * TOK]).then_inc(kv_sb, 1)

            def exp(g, j):
                act.wait_ge(shifted, PAIRS * g + j + 1)
                nc.scalar.activation(ex[:, j].rearrange("p a b -> p (a b)"), sm[:, j].rearrange("p a b -> p (a b)"),
                                     ACT.Exp, scale=HD ** -0.5).then_inc(exped, 1)

            def pt_copy(g, j):
                act.wait_ge(pt_ps, PAIRS * g + j + 1)
                copy(PT[:, j].rearrange("p a b c -> p (a b c)"), PTB[:]).then_inc(pt_sb, 1)

            def ctx_copy(g, j):
                act.wait_ge(ctx_ps, PAIRS * g + j + 1)
                copy(cT[:, :, 2 * j:2 * j + 2, :].rearrange("p h s t -> p s h t"),
                     CTX[:, 0:2 * P].rearrange("p (s h t) -> p s h t", s=2, h=PH)).then_inc(ctx_sb, 1)

            def x1_cols(g, t):
                act.wait_ge(x1T_ps, TT * g + t + 1)
                copy(x1T[:, t].rearrange("p k n -> p (k n)"), TB[t][:]).then_inc(x1T_sb, 1)

            def gate_exp(g):
                act.wait_ge(g_step, 10 * g + 2)
                nc.scalar.activation(le[:].rearrange("p t e -> p (t e)"), lm[:].rearrange("p t e -> p (t e)"),
                                     ACT.Exp).then_inc(g_exp, 1)

            def mgT_copy(g):
                for t in range(TT):
                    act.wait_ge(mgT_ps, TT * g + t + 1)
                    copy(mgT[:, t], TB[t][0:E * R, 0:P]).then_inc(mgT_sb, 1)

            def front(g):
                x_cols(g)
                y_cols(g, 0)
                y_cols(g, 1)
                q_cols(g, 0)
                q_cols(g, 1)
                kv_cols(g)

            def both(a, b):
                if a is not None:
                    lay_adapters(a)
                    x_cols(a)
                    y_cols(a, 0)
                pt_copy(b, 0)
                exp(b, 2)
                if a is not None:
                    y_cols(a, 1)
                ctx_copy(b, 0)
                lay_labels(b)
                pt_copy(b, 1)
                exp(b, 3)
                if a is not None:
                    q_cols(a, 0)
                ctx_copy(b, 1)
                pt_copy(b, 2)
                if a is not None:
                    q_cols(a, 1)
                ctx_copy(b, 2)
                pt_copy(b, 3)
                if a is not None:
                    kv_cols(a)
                ctx_copy(b, 3)
                x1_cols(b, 0)
                x1_cols(b, 1)
                gate_exp(b)
                if a is not None:
                    exp(a, 0)
                mgT_copy(b)
                if a is not None:
                    exp(a, 1)

            act.wait_ge(d_b, 16)
            for k in range(KT):
                act.wait_ge(w_ps, k + 1)
                copy(WT[:, k], bank[3 + k][:]).then_inc(w_sb, 1)
            x_cols(0)
            lay_adapters(0)
            y_cols(0, 0)
            y_cols(0, 1)
            q_cols(0, 0)
            q_cols(0, 1)
            kv_cols(0)
            act.wait_ge(w_ps, KT + 2)
            copy(RAT[:].rearrange("p c n -> p (c n)"), OUT[:, 0:KT * EW]).then_inc(w_sb, 1)
            act.wait_ge(w_ps, KT + 3)
            copy(RT[:].rearrange("p c n -> p (c n)"), PTB[:, 0:KT * EW]).then_inc(w_sb, 1)
            copy(C4[:], PTB[:, KT * EW:(KT + 1) * EW]).then_inc(w_sb, 1)
            act.wait_ge(w_ps, KT + 4)
            nc.scalar.mul(BT[:].rearrange("q (p k) -> q k p", k=KT),
                          CTX[0:E * R].rearrange("q (k p) -> q k p", k=KT), 4.0).then_inc(w_sb, 1)
            exp(0, 0)
            exp(0, 1)
            with act.Fori(0, G - 1) as g:
                both(g + 1, g)
            both(None, G - 1)

        @block.gpsimd
        def _(pool):
            pool.dma_start(W2[:], w2.rearrange("(c p) i -> p c i", p=P)).then_inc(d_w2, 16)
            for g in range(NG):
                pool.dma_start(Wo[HD * g:HD * (g + 1)], wo.rearrange("(g h d) n -> g d h n", g=NG, h=PH)[g]).then_inc(d_o, 16)

            def norm(g, j):
                pool.wait_ge(recip, PAIRS * g + j + 1)
                nc.gpsimd.tensor_tensor(pr[:, j].rearrange("p a b (g t) -> p (a b g) t", t=T), ex[:, j],
                                        ri[:, j, :, None].broadcast_to((P, 2 * NG, T)), ALU.mult).then_inc(normed, 1)

            def times_cos(dst, src, n):
                return nc.gpsimd.tensor_tensor(dst, src, CS[:, 0, None, :].broadcast_to((P, n, T)), ALU.mult)

            def q_times_cos(g, h):
                pool.wait_ge(q_sb, 2 * g + h + 1)
                s = slice(2 * h, 2 * h + 2)
                times_cos(qkc[:, s].rearrange("p h (s t) -> p (h s) t", t=T),
                          qk[:, s].rearrange("p h (s t) -> p (h s) t", t=T), 2 * SEQ).then_inc(q_cos, 1)

            def k_times_cos(g):
                pool.wait_ge(kv_sb, 2 * g + 1)
                times_cos(qkc[:, PH].rearrange("p (s t) -> p s t", t=T),
                          qk[:, PH].rearrange("p (s t) -> p s t", t=T), SEQ).then_inc(k_cos, 1)

            def k_sum(g):
                pool.wait_ge(k_sin, g + 1)
                pool.wait_ge(k_cos, g + 1)
                nc.gpsimd.tensor_tensor(kr[:], qkc[:, PH], qks[:, PH], ALU.add).then_inc(k_rope, 1)

            def q_sum(g, h):
                pool.wait_ge(q_sin, 2 * g + h + 1)
                pool.wait_ge(q_cos, 2 * g + h + 1)
                s = slice(2 * h, 2 * h + 2)
                nc.gpsimd.tensor_tensor(qr[:, :, s, :].rearrange("p s h t -> p h s t"),
                                        qkc[:, s].rearrange("p h (s t) -> p h s t", t=T),
                                        qks[:, s].rearrange("p h (s t) -> p h s t", t=T), ALU.add).then_inc(q_rope, 1)

            def k_blocks(g, j):
                if j == 0:
                    pool.wait_ge(k_rope, g + 1)
                for s in (2 * j, 2 * j + 1):
                    i = nc.gpsimd.tensor_tensor(Kbd[:, s], kr[:, None, T * s:T * (s + 1)].broadcast_to((P, NG, T)),
                                                K[:, C_KG:C_KG + NG, None].broadcast_to((P, NG, T)), ALU.mult)
                i.then_inc(kbd_sb, 1)

            def rope(g):
                k_sum(g)
                k_blocks(g, 0)
                q_sum(g, 0)
                q_sum(g, 1)
                for j in range(1, PAIRS):
                    k_blocks(g, j)

            pool.wait_ge(w_sb, KT + 1)
            k_times_cos(0)
            q_times_cos(0, 0)
            q_times_cos(0, 1)
            rope(0)
            norm(0, 0)
            with pool.Fori(0, G - 1) as g:
                norm(g, 1)
                norm(g, 2)
                norm(g, 3)
                q_times_cos(g + 1, 0)
                q_times_cos(g + 1, 1)
                k_times_cos(g + 1)
                rope(g + 1)
                norm(g + 1, 0)
            for j in range(1, PAIRS):
                norm(G - 1, j)

        @block.vector
        def _(dve):
            V = nc.vector

            def adapter_mask(g):
                dve.wait_ge(h_ps, g + 1)
                V.tensor_tensor(hT[:].rearrange("p (s t) -> p s t", t=T), SMALL[:, 0:TOK].rearrange("p (s t) -> p s t", t=T),
                                K[:, C_SLOT:C_SLOT + SEQ, None].broadcast_to((P, SEQ, T)), ALU.mult).then_inc(h_sb, 1)

            def shift(g, j):
                dve.wait_ge(sc_ps, PAIRS * g + j + 1)
                V.tensor_tensor(sm[:, j], SC[j % 2][:].rearrange("p (a s) -> p a s", s=T),
                                K[:, None, C_CAUSAL:C_CAUSAL + T].broadcast_to((P, 2 * NG, T)), ALU.add).then_inc(masked, 1)
                dve.wait_ge(masked, PAIRS * g + j + 1)
                V.tensor_reduce(mx[:, j], sm[:, j], AX.X, ALU.max).then_inc(maxed, 1)
                dve.wait_ge(maxed, PAIRS * g + j + 1)
                V.tensor_tensor(sm[:, j], sm[:, j], mx[:, j, :, None].broadcast_to((P, 2 * NG, T)),
                                ALU.subtract).then_inc(shifted, 1)

            def sums(g, j):
                dve.wait_ge(exped, PAIRS * g + j + 1)
                V.tensor_reduce(su[:, j], ex[:, j], AX.X, ALU.add).then_inc(summed, 1)
                dve.wait_ge(summed, PAIRS * g + j + 1)
                V.reciprocal(ri[:, j], su[:, j]).then_inc(recip, 1)

            def times_sin(dst, src, n):
                return V.tensor_tensor(dst, src, CS[:, 1, None, :].broadcast_to((P, n, T)), ALU.mult)

            def k_times_sin(g):
                dve.wait_ge(rotk_ps, g + 1)
                times_sin(qks[:, PH].rearrange("p (s t) -> p s t", t=T),
                          SMALL[:, 0:TOK].rearrange("p (s t) -> p s t", t=T), SEQ).then_inc(k_sin, 1)

            def q_times_sin(g, h):
                dve.wait_ge(rotq_ps, 2 * g + h + 1)
                times_sin(qks[:, 2 * h:2 * h + 2].rearrange("p h (s t) -> p (h s) t", t=T),
                          FR[h][:].rearrange("p (a t) -> p a t", t=T), 2 * SEQ).then_inc(q_sin, 1)

            def v_blocks(g, t):
                dve.wait_ge(vr_ps, TT * g + t + 1)
                for half in range(2):
                    V.tensor_tensor(Vbd[:, half, 4 * t:4 * t + 4].rearrange("p s (g d) -> p s g d", d=HD),
                                    SMALL[:].rearrange("p (s g d) -> p s g d", s=4, d=HD),
                                    K[:, None, C_VG + NG * half:C_VG + NG * (half + 1), None].broadcast_to((P, 4, NG, HD)),
                                    ALU.mult).then_inc(vbd_sb, 1)

            def residual(g, t):
                dve.wait_ge(wo_ps, TT * g + t + 1)
                dve.wait_ge(d_xres, 16 * (TT * g + TT))
                V.tensor_tensor(x1[:, t], TB[t][:], xres[:, t], ALU.add).then_inc(x1_sb, 1)

            def label_mask(g, t):
                dve.wait_ge(low_ps, TT * g + t + 1)
                V.tensor_tensor(lT[:, t].rearrange("p (s t) -> p s t", t=T), TB[t][:, 0:P].rearrange("p (s t) -> p s t", t=T),
                                K[:, C_LABEL:C_LABEL + 4, None].broadcast_to((P, 4, T)), ALU.mult).then_inc(low_sb, 1)

            def gates(g):
                def step(n, ins):
                    ins.then_inc(g_step, 1)
                    dve.wait_ge(g_step, 10 * g + n)

                for t in range(TT):
                    dve.wait_ge(mid_ps, TT * g + t + 1)
                    V.tensor_copy(mid[:, t], TB[t][:, 0:EW]).then_inc(mid_sb, 1)
                dve.wait_ge(mid_sb, TT * g + TT)
                lg = mid[:, :, E * R:EW]
                of_j, of_e = lg[:, :, None, :].broadcast_to((P, TT, E, E)), lg[:, :, :, None].broadcast_to((P, TT, E, E))
                step(1, V.tensor_reduce(m1[:], lg, AX.X, ALU.max))
                step(2, V.tensor_tensor(lm[:], lg, m1[:, :, None].broadcast_to((P, TT, E)), ALU.subtract))
                step(3, V.tensor_tensor(eq[:], of_j, of_e, ALU.is_equal))
                step(4, V.tensor_tensor(eq[:], eq[:], K[:, None, C_TRI:C_TRI + E * E].rearrange("p a (e j) -> p a e j", e=E)
                                        .broadcast_to((P, TT, E, E)), ALU.mult))
                step(5, V.tensor_tensor(gt[:], of_j, of_e, ALU.is_gt))
                step(6, V.tensor_tensor(gt[:], gt[:], eq[:], ALU.add))
                step(7, V.tensor_reduce(rk[:], gt[:], AX.X, ALU.add))
                dve.wait_ge(g_exp, g + 1)
                step(8, V.scalar_tensor_tensor(out=gw[:], in0=rk[:], scalar=1.5, in1=le[:], op0=ALU.is_lt, op1=ALU.mult))
                step(9, V.tensor_reduce(gs[:], gw[:], AX.X, ALU.add))
                step(10, V.reciprocal(gr[:], gs[:]))
                V.tensor_tensor(gate[:], gw[:], gr[:, :, None].broadcast_to((P, TT, E)), ALU.mult).then_inc(g_mid, 1)
                dve.wait_ge(g_mid, (TT + 1) * g + 1)
                for t in range(TT):
                    V.tensor_tensor(mg[:, t, 0:E * R].rearrange("p (e r) -> p e r", e=E), mid[:, t, 0:E * R].rearrange("p (e r) -> p e r", e=E),
                                    gate[:, t, :, None].broadcast_to((P, E, R)), ALU.mult).then_inc(g_mid, 1)

            def finish(g):
                for t in range(TT):
                    dve.wait_ge(dl_ps, TT * g + t + 1)
                    if not (isinstance(g, int) and g == 0):
                        dve.wait_ge(d_out, 16 * TT * g)
                    V.tensor_tensor(fin[:, t], TB[t][:], x1[:, t], ALU.add).then_inc(fin_sb, 1)

            def both(a, b):
                sums(b, 1)
                if a is not None:
                    adapter_mask(a)
                shift(b, 2)
                shift(b, 3)
                sums(b, 2)
                sums(b, 3)
                if a is not None:
                    k_times_sin(a)
                residual(b, 0)
                if a is not None:
                    q_times_sin(a, 0)
                    q_times_sin(a, 1)
                residual(b, 1)
                if a is not None:
                    v_blocks(a, 0)
                label_mask(b, 0)
                if a is not None:
                    v_blocks(a, 1)
                label_mask(b, 1)
                gates(b)
                if a is not None:
                    shift(a, 0)
                    shift(a, 1)
                finish(b)
                if a is not None:
                    sums(a, 0)

            V.memset(mg[:], 0.0)
            dve.wait_ge(d_cs, 32)
            V.tensor_copy(cs8[:], cs[:, :, None, :].broadcast_to((T, 2, NG, HD))).then_inc(cs_laid, 1)
            dve.wait_ge(d_K, 16)
            V.tensor_copy(spread[:], ident.rearrange("p (s t) -> p s t", s=4)[:, :, None, :].broadcast_to((P, 4, 4, T))).then_inc(spread_laid, 1)
            dve.wait_ge(w_ps, KT + 1)
            V.tensor_copy(CS[:].rearrange("p a t -> p (a t)"), bank[7][:, 0:2 * T]).then_inc(w_sb, 1)
            dve.wait_ge(d_bw, 16)
            V.tensor_copy(Bw4[:], Bw[:, :, None, :].broadcast_to((P, KT, 4, R2))).then_inc(bw_laid, 1)
            dve.wait_ge(d_bf, 16)
            V.tensor_copy(Bk[:], Bf[:].rearrange("p e k r -> p k e r")).then_inc(bf_laid, 1)
            adapter_mask(0)
            dve.wait_ge(d_q, 16)
            for c in range(KT):
                V.tensor_copy(Wq[:, c].rearrange("p h (g d) -> p h g d", g=NG),
                              Wqn[:, c].rearrange("p (g h d) -> p h g d", g=NG, h=PH)).then_inc(wq_laid, 1)
            k_times_sin(0)
            q_times_sin(0, 0)
            q_times_sin(0, 1)
            v_blocks(0, 0)
            v_blocks(0, 1)
            shift(0, 0)
            shift(0, 1)
            sums(0, 0)
            both(1, 0)
            with dve.Fori(1, G - 1) as g:
                both(g + 1, g)
            both(None, G - 1)

        @block.tensor
        def _(pe):
            def mm(dst, lhsT, rhs, start, stop):
                return nc.tensor.matmul(dst, lhsT, rhs, start=start, stop=stop)

            def tr(dst, src, n=P):
                return nc.tensor.transpose(dst, src, ident[0:n, 0:n])

            def x_transposes(g):
                pe.wait_ge(d_x, 16 * (TT * g + TT))
                for h in range(2):
                    for k in (2 * h, 2 * h + 1):
                        for t in range(TT):
                            c = (k % 2) * TOK + t * P
                            i = tr(FR[h][:, c:c + P], xin[:, t, k:D:KT])
                    i.then_inc(xT_ps, 1)

            def adapter_in(g):
                pe.wait_ge(xT_sb, 2 * g + 2)
                pe.wait_ge(a1_laid, g + 1)
                for k in range(KT):
                    i = mm(SMALL[:, 0:TOK], A1[:, k].rearrange("p s r -> p (s r)"), xT[:, k], k == 0, k == KT - 1)
                i.then_inc(h_ps, 1)

            def y_tiles(g, h):
                for c in (2 * h, 2 * h + 1):
                    dst = FR[h][:, (c % 2) * TOK:(c % 2 + 1) * TOK]
                    for k in range(KT):
                        mm(dst, WT[:, k, P * c:P * (c + 1)], xT[:, k], k == 0, False)
                    if c == 0:
                        pe.wait_ge(h_sb, g + 1)
                    i = mm(dst, B1[:, P * c:P * (c + 1)], hT[:], False, True)
                i.then_inc(y_ps, 1)

            def q_tiles(g, h):
                if h == 0:
                    pe.wait_ge(y_sb, KT * (g + 1))
                for q in (2 * h, 2 * h + 1):
                    dst = FR[h][:, (q % 2) * TOK:(q % 2 + 1) * TOK]
                    for c in range(KT):
                        i = mm(dst, Wq[:, c, q], yT[:, c], c == 0, c == KT - 1)
                i.then_inc(q_ps, 1)

            def kv_tiles(g):
                for c in range(KT):
                    mm(SMALL[:, 0:TOK], Wk[:, c], yT[:, c], c == 0, c == KT - 1)
                for t in range(TT):
                    for c in range(KT):
                        i = mm(SMALL[:, TOK + P * t:TOK + P * (t + 1)], yT[:, c, P * t:P * (t + 1)], Wv[:, c],
                               c == 0, c == KT - 1)
                i.then_inc(kv_ps, 1)

            def rotate_k(g):
                pe.wait_ge(kv_sb, 2 * g + 2)
                mm(SMALL[:, 0:TOK], rot, qk[:, PH], True, True).then_inc(rotk_ps, 1)

            def rotate_q(g):
                for h in range(2):
                    pe.wait_ge(q_sb, 2 * g + h + 1)
                    mm(FR[h][:], rot, qk[:, 2 * h:2 * h + 2].rearrange("p h t -> p (h t)"), True, True).then_inc(rotq_ps, 1)

            def v_spread(g, t):
                if t == 0:
                    pe.wait_ge(k_sin, g + 1)
                else:
                    pe.wait_ge(vbd_sb, 2 * TT * g + 2)
                for s in range(4):
                    i = mm(SMALL[:, P * s:P * (s + 1)],
                           spread[:, s].rearrange("p a t -> p (a t)"), v[:, t], True, True)
                i.then_inc(vr_ps, 1)

            def scores(g, j):
                if j < 2:
                    pe.wait_ge(q_rope, 2 * g + 2)
                    if not (isinstance(g, int) and g == 0):
                        pe.wait_ge(masked, PAIRS * g - 2 + j + 1)
                else:
                    pe.wait_ge(masked, PAIRS * g + j - 1)
                pe.wait_ge(kbd_sb, PAIRS * g + j + 1)
                for s in range(2):
                    i = mm(SC[j % 2][:, 2 * P * s:2 * P * (s + 1)], qr[:, 2 * j + s].rearrange("p h t -> p (h t)"),
                           Kbd[:, 2 * j + s].rearrange("p g t -> p (g t)"), True, True)
                i.then_inc(sc_ps, 1)

            def p_transposes(g, j):
                pe.wait_ge(normed, PAIRS * g + j + 1)
                if j > 0:
                    pe.wait_ge(pt_sb, PAIRS * g + j)
                for s in range(2):
                    for half in range(2):
                        c = (2 * s + half) * P
                        i = tr(PTB[:, c:c + P], pr[:, j, s, half])
                i.then_inc(pt_ps, 1)

            def context(g, j):
                pe.wait_ge(pt_sb, PAIRS * g + j + 1)
                if j == 0:
                    pe.wait_ge(vbd_sb, 2 * TT * (g + 1))
                else:
                    pe.wait_ge(ctx_sb, PAIRS * g + j)
                for s in range(2):
                    for half in range(2):
                        i = mm(CTX[:, P * s:P * (s + 1)], Vbd[:, half, 2 * j + s], PT[:, j, s, half], half == 0, half == 1)
                i.then_inc(ctx_ps, 1)

            def project(g, t):
                pe.wait_ge(ctx_sb, PAIRS * g + 2 * (t + 1))
                for h in range(PH):
                    i = mm(TB[t][:], cT[:, h, 4 * t:4 * t + 4].rearrange("p s t -> p (s t)"), Wo[:, h], h == 0, h == PH - 1)
                i.then_inc(wo_ps, 1)

            def x1_transposes(g, t):
                pe.wait_ge(x1_sb, TT * g + t + 1)
                for k in range(KT):
                    i = tr(TB[t][:, P * k:P * (k + 1)], x1[:, t, k:D:KT])
                i.then_inc(x1T_ps, 1)

            def label_in(g, t):
                pe.wait_ge(x1T_sb, TT * g + t + 1)
                pe.wait_ge(a2_laid, g + 1)
                for k in range(KT):
                    i = mm(TB[t][:, 0:P], A2[:, k, 4 * t:4 * t + 4].rearrange("p s r -> p (s r)"), x1T[:, t, k], k == 0, k == KT - 1)
                i.then_inc(low_ps, 1)

            def mid_logits(g, t):
                pe.wait_ge(low_sb, TT * g + t + 1)
                for k in range(KT):
                    mm(TB[t][:, 0:EW], x1T[:, t, k], RT[:, k], k == 0, False)
                mm(TB[t][:, 0:EW], lT[:, t], C4[:], False, True).then_inc(mid_ps, 1)

            def mid_transposes(g):
                for t in range(TT):
                    pe.wait_ge(g_mid, (TT + 1) * g + t + 2)
                    tr(TB[t][:, 0:P], mg[:, t]).then_inc(mgT_ps, 1)

            def deltas(g):
                for t in range(TT):
                    pe.wait_ge(mgT_sb, TT * g + t + 1)
                    mm(TB[t][:], mgT[:, t], BT[:], True, True).then_inc(dl_ps, 1)

            def both(a, b, first=False):
                if a is not None:
                    if not first:
                        pass
                    x_transposes(a)
                    adapter_in(a)
                    y_tiles(a, 0)
                if not first:
                    pe.wait_ge(fin_sb, TT * b)
                p_transposes(b, 0)
                scores(b, 2)
                if a is not None:
                    y_tiles(a, 1)
                context(b, 0)
                p_transposes(b, 1)
                scores(b, 3)
                if a is not None:
                    q_tiles(a, 0)
                context(b, 1)
                p_transposes(b, 2)
                if a is not None:
                    q_tiles(a, 1)
                context(b, 2)
                p_transposes(b, 3)
                if a is not None:
                    kv_tiles(a)
                context(b, 3)
                if a is not None:
                    rotate_k(a)
                project(b, 0)
                if a is not None:
                    rotate_q(a)
                project(b, 1)
                x1_transposes(b, 0)
                if a is not None:
                    v_spread(a, 0)
                x1_transposes(b, 1)
                label_in(b, 0)
                if a is not None:
                    v_spread(a, 1)
                label_in(b, 1)
                mid_logits(b, 0)
                mid_logits(b, 1)
                if a is not None:
                    scores(a, 0)
                    scores(a, 1)
                mid_transposes(b)
                deltas(b)

            pe.wait_ge(d_K, 16)
            pe.wait_ge(d_W, 16)
            for k in range(KT):
                for c in range(KT):
                    i = tr(bank[3 + k][:, P * c:P * (c + 1)], Wn[:, c, k:D:KT])
                i.then_inc(w_ps, 1)
            pe.wait_ge(cs_laid, 1)
            for a in range(2):
                i = mm(bank[7][:, T * a:T * (a + 1)], cs8[:, a].rearrange("t g d -> t (g d)"), ident[0:T, 0:T], True, True)
            i.then_inc(w_ps, 1)
            x_transposes(0)
            adapter_in(0)
            pe.wait_ge(w_sb, KT + 1)
            y_tiles(0, 0)
            y_tiles(0, 1)
            pe.wait_ge(wq_laid, KT)
            q_tiles(0, 0)
            q_tiles(0, 1)
            pe.wait_ge(d_k, 16)
            pe.wait_ge(d_v, 16)
            kv_tiles(0)
            rotate_k(0)
            rotate_q(0)
            pe.wait_ge(d_ra, 32)
            for c in range(KT):
                i = tr(OUT[:, EW * c:EW * (c + 1)], RA[:, P * c:P * (c + 1)], EW)
            i.then_inc(w_ps, 1)
            pe.wait_ge(spread_laid, 1)
            v_spread(0, 0)
            v_spread(0, 1)
            pe.wait_ge(w_sb, KT + 2)
            pe.wait_ge(d_w2, 16)
            for k in range(KT):
                for c in range(KT):
                    mm(PTB[:, EW * k:EW * (k + 1)], W2[:, c, k:D:KT], RAT[:, c], c == 0, c == KT - 1)
            pe.wait_ge(bw_laid, 1)
            for c in range(KT):
                i = mm(PTB[:, EW * KT:EW * (KT + 1)], Bw4[:, c].rearrange("p a r -> p (a r)"), RAT[:, c], c == 0, c == KT - 1)
            i.then_inc(w_ps, 1)
            pe.wait_ge(bf_laid, 1)
            for c in range(KT):
                i = tr(CTX[0:E * R, P * c:P * (c + 1)], Bk[:, c].rearrange("p e r -> p (e r)"))
            i.then_inc(w_ps, 1)
            scores(0, 0)
            scores(0, 1)
            pe.wait_ge(w_sb, KT + 5)
            pe.wait_ge(d_o, 16 * NG)
            both(1, 0, first=True)
            with pe.Fori(1, G - 1) as g:
                both(g + 1, g)
            both(None, G - 1)


_INS = ["x", "itok_B_0_23", "itok_B_0_2", "L0_cond_W", "L0_cond_b", "L0_cond_lora_As", "L0_cond_lora_Bs",
        "L0_attn_Wq", "L0_attn_Wk", "L0_attn_Wv", "L0_attn_Wo", "L0_attn_cos", "L0_attn_sin",
        "L0_cond2_W", "L0_cond2_lora_A", "L0_cond2_lora_B_w", "L0_ffn_router_w", "L0_ffn_A", "L0_ffn_B"]


def kernel(**inputs):
    import concourse.bacc as bacc
    from concourse.bass_utils import run_bass_kernel_spmd

    nc = bacc.Bacc("TRN2", target_bir_lowering=False, num_devices=1)
    arrays, args = {}, []
    for name in _INS:
        a = np.ascontiguousarray(inputs[name])
        arrays[name] = a
        args.append(nc.dram_tensor(name, a.shape, mybir.dt.from_np(a.dtype), kind="ExternalInput").ap())
    arrays["constants"] = shape_constants()
    args.append(nc.dram_tensor("constants", (P, C_N), F32, kind="ExternalInput").ap())
    args.append(nc.dram_tensor("out", (B, T, D), F32, kind="ExternalOutput").ap())
    program(nc, *args)
    r = run_bass_kernel_spmd(nc, [arrays], core_ids=[0])
    return r.results[0]["out"]
```

```python
from contextlib import ExitStack

import numpy as np
import concourse.bass as bass
from concourse import mybir

F32 = mybir.dt.float32
F32R = mybir.dt.float32r
I32 = mybir.dt.int32
ALU = mybir.AluOpType
ACT = mybir.ActivationFunctionType
AX = mybir.AxisListType

P = 128
B, T, D = 32, 32, 512
KT = D // P
G = 4
SEQ = B // G
TOK = SEQ * T
TT = TOK // P
HD, NG, PH = 16, 8, 4
R1, R2 = 16, 32
SLOTS, LABELS = 32, 5
E, R = 4, 16
EW = E * R + E
PAIRS = SEQ // 2
NEG = -3.0e38
POOL_SLOTS = 3

C_ID, C_ROT, C_CAUSAL, C_KG, C_SLOT, C_LABEL, C_VG, C_TRI, C_N = 0, 128, 256, 288, 296, 304, 308, 324, 340


def shape_constants():
    c = np.zeros((P, C_N), np.float32)
    p = np.arange(P)
    c[:, C_ID:C_ID + P] = np.eye(P)
    for m in range(P):
        if m % HD < HD // 2:
            c[m + HD // 2, C_ROT + m] = -1
        else:
            c[m - HD // 2, C_ROT + m] = 1
    c[:, C_CAUSAL:C_CAUSAL + T] = np.where(np.arange(T)[None] <= (p % T)[:, None], 0, NEG)
    c[:, C_KG:C_KG + NG] = (p // HD)[:, None] == np.arange(NG)
    c[:, C_SLOT:C_SLOT + SEQ] = 2.0 * ((p // R1)[:, None] == np.arange(SEQ))
    c[:, C_LABEL:C_LABEL + 4] = 0.5 * ((p // R2)[:, None] == np.arange(4))
    for half in range(2):
        c[:, C_VG + NG * half:C_VG + NG * (half + 1)] = (p // T + 4 * half)[:, None] == np.arange(NG)
    c[:, C_TRI:C_TRI + E * E] = (np.arange(E)[None, :] < np.arange(E)[:, None]).reshape(-1)
    return c


def program(nc, x, slot_ids, label_ids, cW, cb, lA, lB, wq, wk, wv, wo, cos, sin, w2, a2, bw, rw, fA, fB, consts, out):
    ctx = ExitStack()
    with ctx:
        def sb(name, shape, dt=F32):
            return ctx.enter_context(nc.sbuf_tensor(name, shape, dt))

        def sem(name):
            return ctx.enter_context(nc.semaphore(name))

        K = sb("K", [P, C_N])
        ids = sb("ids", [1, 2, B], I32)
        Wn = sb("Wn", [P, KT, D])
        W2 = Wn
        WT = [sb(f"WT{i}", [P, KT, D], F32R) for i in "hl"]
        bias = sb("bias", [P, KT])
        Wqn = sb("Wqn", [P, KT, D])
        Wq = [sb(f"Wq{i}", [P, KT, PH, P], F32R) for i in "hl"]
        Wkn = sb("Wkn", [P, KT, P])
        Wk = [sb(f"Wk{i}", [P, KT, P], F32R) for i in "hl"]
        Wv = sb("Wv", [P, KT, P])
        Won = Wqn
        Wo = [sb(f"Wo{i}", [P, PH, D], F32R) for i in "hl"]
        Bw = sb("Bw", [P, KT, R2])
        Bw4 = sb("Bw4", [P, KT, 4, R2])
        RA = sb("RA", [EW, D])
        RAT = sb("RAT", [P, KT, EW])
        RT = sb("RT", [P, KT, EW])
        C4 = sb("C4", [P, EW])
        Bf = sb("Bf", [P, E, KT, R])
        Bk = sb("Bk", [P, KT, E, R])
        BT = sb("BT", [E * R, D])
        cs = sb("cs", [T, 2, HD])
        cs8 = sb("cs8", [T, 2, NG, HD])
        spread = sb("spread", [P, 4, 4, T])
        CS = sb("CS", [P, 2, T])
        xin = sb("xin", [P, TT, D])
        A1n = sb("A1n", [P, SEQ, KT, R1])
        A1 = [sb(f"A1{i}", [P, KT, SEQ, R1], F32R) for i in "hl"]
        B1 = sb("B1", [P, D])
        xT = [sb(f"xT{i}", [P, KT, TOK], F32R) for i in "hl"]
        hT = sb("hT", [P, TOK])
        yT = sb("yT", [P, KT, TOK])
        yS = [sb(f"yT{i}", [P, KT, TOK], F32R) for i in "hl"]
        qk = sb("qk", [P, PH + 1, TOK])
        qkc = sb("qkc", [P, PH + 1, TOK])
        qks = sb("qks", [P, PH + 1, TOK])
        qr = sb("qr", [P, SEQ, PH, T])
        kr = sb("kr", [P, TOK])
        Kbd = sb("Kbd", [P, SEQ, NG, T])
        v = sb("v", [P, TT, P])
        Vbd = sb("Vbd", [P, 2, SEQ, P])
        sm = sb("sm", [P, 2, 2 * NG, T])
        mx = sb("mx", [P, PAIRS, 2 * NG])
        ex = sb("ex", [P, PAIRS, 2 * NG, T])
        su = sb("su", [P, PAIRS, 2 * NG])
        ri = sb("ri", [P, PAIRS, 2 * NG])
        PT = sb("PT", [P, 2, 2, 2, P])
        cT = [sb(f"cT{i}", [P, PH, SEQ, T], F32R) for i in "hl"]
        xres = sb("xres", [P, TT, D])
        x1 = sb("x1", [P, TT, D])
        x1T = sb("x1T", [P, TT, KT, P])
        A2n = sb("A2n", [P, SEQ, KT, R2])
        A2 = sb("A2", [P, KT, SEQ, R2])
        lT = sb("lT", [P, TT, P])
        mid = sb("mid", [P, TT, EW])
        m1 = sb("m1", [P, TT])
        lm = sb("lm", [P, TT, E])
        gt = sb("gt", [P, TT, E, E])
        eq = sb("eq", [P, TT, E, E])
        rk = sb("rk", [P, TT, E])
        le = sb("le", [P, TT, E])
        gw = sb("gw", [P, TT, E])
        gs = sb("gs", [P, TT])
        gr = sb("gr", [P, TT])
        gate = sb("gate", [P, TT, E])
        mg = sb("mg", [P, TT, P])
        mgT = sb("mgT", [E * R, TT, P])

        bank = [ctx.enter_context(nc.psum_tensor(f"bank{i}", [P, 512], F32)) for i in range(8)]
        FR, SMALL, SC, PTB, CTX, OUT = bank[0:2], bank[2], bank[3:5], bank[5], bank[6], bank[7]
        TB = [OUT, PTB]
        LB = SC

        d_ids, d_K, d_cs, d_b, d_q, d_k, d_v, d_o, d_w2, d_bw, d_ra, d_bf = map(
            sem, "d_ids d_K d_cs d_b d_q d_k d_v d_o d_w2 d_bw d_ra d_bf".split())
        d_x, d_slot, d_xres, d_a2, d_out = map(sem, "d_x d_slot d_xres d_a2 d_out".split())
        d_W = [sem(f"d_W{c}") for c in range(KT)]
        d_slot_pool = sem("d_slot_pool")
        WT_ps, RAT_ps, RAT_sb, CS_ps, CS_sb, RT_ps, RT_sb, C4_ps, C4_sb, BT_ps, BT_sb, zeroed = map(
            sem, "WT_ps RAT_ps RAT_sb CS_ps CS_sb RT_ps RT_sb C4_ps C4_sb BT_ps BT_sb zeroed".split())
        WT_h, WT_l, Wq_h, Wk_h, Wk_l, Wo_h, Wo_l, A1_l, xT_l, yT_h, yT_l, cT_l = map(
            sem, "WT_h WT_l Wq_h Wk_h Wk_l Wo_h Wo_l A1_l xT_l yT_h yT_l cT_l".split())
        cs_laid, spread_laid, wq_laid, bw_laid, bf_laid, a1_laid, a2_laid = map(
            sem, "cs_laid spread_laid wq_laid bw_laid bf_laid a1_laid a2_laid".split())
        xT_ps, xT_sb, h_ps, h_sb, y_ps, y_sb, q_ps, q_sb, kv_ps, kv_sb = map(
            sem, "xT_ps xT_sb h_ps h_sb y_ps y_sb q_ps q_sb kv_ps kv_sb".split())
        rotk_ps, rotq_ps, k_sin, q_sin, k_cos, q_cos, k_rope, q_rope, kbd_sb, vr_ps, vbd_sb = map(
            sem, "rotk_ps rotq_ps k_sin q_sin k_cos q_cos k_rope q_rope kbd_sb vr_ps vbd_sb".split())
        sc_ps, masked, maxed, shifted, exped, summed, recip, normed, pt_ps, pt_sb, ctx_ps, ctx_sb = map(
            sem, "sc_ps masked maxed shifted exped summed recip normed pt_ps pt_sb ctx_ps ctx_sb".split())
        wo_ps, x1_sb, x1T_ps, x1T_sb, low_ps, low_sb, mid_ps, mid_sb = map(
            sem, "wo_ps x1_sb x1T_ps x1T_sb low_ps low_sb mid_ps mid_sb".split())
        g_step, g_exp, gated, g_mid, mgT_ps, mgT_sb, dl_ps, fin_sb = map(
            sem, "g_step g_exp gated g_mid mgT_ps mgT_sb dl_ps fin_sb".split())

        ident = K[:, C_ID:C_ID + P]
        rot = K[:, C_ROT:C_ROT + P]

        def load_slots(eng, g, seqs=range(SEQ), arrived=d_slot):
            for s in seqs:
                slot = eng.value_load(ids[0:1, 0, bass.ds(g * SEQ + s, 1)], min_val=0, max_val=SLOTS - 1)
                eng.dma_start(A1n[:, s].rearrange("p k r -> p (k r)"),
                              lA[bass.ds(slot, 1)].rearrange("a (p k) r -> p (a k r)", k=KT)).then_inc(arrived, 16)
                eng.dma_start(B1[R1 * s:R1 * (s + 1), :],
                              lB[bass.ds(slot, 1)].rearrange("a r o -> (a r) o")).then_inc(arrived, 16)

        block = ctx.enter_context(nc.Block())

        @block.sync
        def _(sp):
            xf = x.rearrange("(g t s) u d -> g t (s u) d", g=G, t=TT)
            of = out.rearrange("(g t s) u d -> g t (s u) d", g=G, t=TT)

            def load_x(g):
                for t in range(TT):
                    sp.dma_start(xin[:, t, :], xf[bass.ds(g, 1), t].rearrange("a p d -> p (a d)")).then_inc(d_x, 16)

            def load_labels(g):
                for s in range(SEQ):
                    label = sp.value_load(ids[0:1, 1, bass.ds(g * SEQ + s, 1)], min_val=0, max_val=LABELS - 1)
                    sp.dma_start(A2n[:, s].rearrange("p k r -> p (k r)"),
                                 a2[bass.ds(label, 1)].rearrange("a (p k) r -> p (a k r)", k=KT)).then_inc(d_a2, 16)

            def load_xres(g):
                for t in range(TT):
                    sp.dma_start(xres[:, t, :], xf[bass.ds(g, 1), t].rearrange("a p d -> p (a d)")).then_inc(d_xres, 16)

            def front_loads(g):
                sp.wait_ge(xT_ps, 2 * g)
                load_x(g)
                sp.wait_ge(A1_l, g)
                sp.wait_ge(y_ps, 2 * g)
                load_slots(sp, g)

            def back_loads(g):
                sp.wait_ge(x1_sb, TT * g)
                load_xres(g)
                sp.wait_ge(a2_laid, g)
                load_labels(g)

            def store(g):
                sp.wait_ge(fin_sb, TT * (g + 1))
                for t in range(TT):
                    sp.dma_start(of[bass.ds(g, 1), t].rearrange("a p d -> p (a d)"), x1[:, t, :]).then_inc(d_out, 16)

            load_x(0)
            sp.dma_start(ids[:, 0], slot_ids.rearrange("(a b) -> a b", a=1)).then_inc(d_ids, 16)
            sp.dma_start(ids[:, 1], label_ids.rearrange("(a b) -> a b", a=1)).then_inc(d_ids, 16)
            sp.wait_ge(d_ids, 32)
            load_slots(sp, 0, range(POOL_SLOTS, SEQ))
            sp.dma_start(bias[:], cb.rearrange("(c p) -> p c", p=P), allow_slow_non_contiguous=True).then_inc(d_b, 16)
            sp.dma_start(RA[0:E * R], fA.rearrange("e r d -> (e r) d")).then_inc(d_ra, 16)
            sp.dma_start(RA[E * R:EW], rw).then_inc(d_ra, 16)
            sp.dma_start(cs[:, 0], cos[0:T, :]).then_inc(d_cs, 16)
            sp.dma_start(cs[:, 1], sin[0:T, :]).then_inc(d_cs, 16)
            sp.wait_ge(WT_ps, KT)
            sp.dma_start(W2[:], w2.rearrange("(c p) i -> p c i", p=P)).then_inc(d_w2, 16)
            sp.dma_start(Wkn[:], wk.rearrange("(c p) n -> p c n", p=P)).then_inc(d_k, 16)
            sp.dma_start(Wv[:], wv.rearrange("(c p) n -> p c n", p=P)).then_inc(d_v, 16)
            sp.dma_start(Bw[:], bw.rearrange("(c p) r -> p c r", p=P)).then_inc(d_bw, 16)
            sp.dma_start(Bf[:].rearrange("p e k r -> p e (k r)"),
                         fB.rearrange("e (p k) r -> p e (k r)", k=KT)).then_inc(d_bf, 16)
            sp.wait_ge(wq_laid, KT)
            for g in range(NG):
                sp.dma_start(Won[HD * g:HD * (g + 1)], wo.rearrange("(g h d) n -> g d h n", g=NG, h=PH)[g]).then_inc(d_o, 16)
            front_loads(1)
            load_xres(0)
            load_labels(0)
            with sp.Fori(0, G - 2) as g:
                front_loads(g + 2)
                back_loads(g + 1)
                store(g)
            back_loads(G - 1)
            store(G - 2)
            for t in range(TT):
                sp.wait_ge(fin_sb, TT * (G - 1) + t + 1)
                sp.dma_start(of[G - 1, t], xres[:, t, :]).then_inc(d_out, 16)
            sp.wait_ge(d_out, 16 * TT * G)

        @block.scalar
        def _(act):
            act.dma_start(K[:], consts).then_inc(d_K, 16)
            for c in range(KT):
                act.dma_start(Wn[:, c], cW[P * c:P * (c + 1)]).then_inc(d_W[c], 16)

            def copy(dst, src):
                return nc.scalar.copy(dst, src)

            def lay_adapters(g):
                act.wait_ge(d_slot, 16 * 2 * (SEQ * (g + 1) - POOL_SLOTS))
                if isinstance(g, int) and g == 0:
                    act.wait_ge(d_slot_pool, 16 * 2 * POOL_SLOTS)
                else:
                    act.wait_ge(h_ps, g)
                copy(A1[0][:].rearrange("p k s r -> p s k r"), A1n[:]).then_inc(a1_laid, 1)

            def lay_labels(g):
                act.wait_ge(d_a2, 16 * SEQ * (g + 1))
                if not (isinstance(g, int) and g == 0):
                    act.wait_ge(low_ps, TT * g)
                copy(A2[:].rearrange("p k s r -> p s k r"), A2n[:]).then_inc(a2_laid, 1)

            def x_cols(g):
                for h in range(2):
                    act.wait_ge(xT_ps, 2 * g + h + 1)
                    copy(xT[0][:, 2 * h:2 * h + 2].rearrange("p k t -> p (k t)"), FR[h][:]).then_inc(xT_sb, 1)

            def y_cols(g, h):
                act.wait_ge(y_ps, 2 * g + h + 1)
                for c in (2 * h, 2 * h + 1):
                    nc.scalar.activation(yT[:, c, :], FR[h][:, (c % 2) * TOK:(c % 2 + 1) * TOK], ACT.Identity,
                                         bias=bias[:, c:c + 1]).then_inc(y_sb, 1)

            def q_cols(g, h):
                act.wait_ge(q_ps, 2 * g + h + 1)
                copy(qk[:, 2 * h:2 * h + 2].rearrange("p k t -> p (k t)"), FR[h][:]).then_inc(q_sb, 1)

            def kv_cols(g):
                act.wait_ge(kv_ps, g + 1)
                copy(qk[:, PH, :], SMALL[:, 0:TOK]).then_inc(kv_sb, 1)
                copy(v[:].rearrange("p t n -> p (t n)"), SMALL[:, TOK:2 * TOK]).then_inc(kv_sb, 1)

            def exp(g, j):
                act.wait_ge(shifted, PAIRS * g + j + 1)
                nc.scalar.activation(ex[:, j].rearrange("p a b -> p (a b)"), sm[:, j % 2].rearrange("p a b -> p (a b)"),
                                     ACT.Exp, scale=HD ** -0.5).then_inc(exped, 1)

            def pt_copy(g, j, src=PTB):
                act.wait_ge(pt_ps, PAIRS * g + j + 1)
                copy(PT[:, j % 2].rearrange("p a b c -> p (a b c)"), src[:]).then_inc(pt_sb, 1)

            def ctx_copy(g, j, src=CTX):
                act.wait_ge(ctx_ps, PAIRS * g + j + 1)
                copy(cT[0][:, :, 2 * j:2 * j + 2, :].rearrange("p h s t -> p s h t"),
                     src[:, 0:2 * P].rearrange("p (s h t) -> p s h t", s=2, h=PH)).then_inc(ctx_sb, 1)

            def x1_cols(g, t, tb=TB):
                act.wait_ge(x1T_ps, TT * g + t + 1)
                copy(x1T[:, t].rearrange("p k n -> p (k n)"), tb[t][:]).then_inc(x1T_sb, 1)

            def gate_exp(g, t=None):
                n, ts = (0, slice(0, TT)) if t is None else (t, slice(t, t + 1))
                act.wait_ge(g_step, 10 * (g + n) + 2)
                nc.scalar.activation(le[:, ts].rearrange("p t e -> p (t e)"), lm[:, ts].rearrange("p t e -> p (t e)"),
                                     ACT.Exp).then_inc(g_exp, 1)

            def mgT_copy(g, t=None, tb=TB):
                for t in range(TT) if t is None else (t,):
                    act.wait_ge(mgT_ps, TT * g + t + 1)
                    copy(mgT[:, t], tb[t][0:E * R, 0:P]).then_inc(mgT_sb, 1)

            def both(a, b, first=False):
                lay_adapters(a)
                x_cols(a)
                exp(b, 0)
                exp(b, 1)
                if not first:
                    gate_exp(b - 1)
                y_cols(a, 0)
                if not first:
                    mgT_copy(b - 1)
                y_cols(a, 1)
                pt_copy(b, 0)
                ctx_copy(b, 0)
                pt_copy(b, 1)
                exp(b, 2)
                q_cols(a, 0)
                ctx_copy(b, 1)
                exp(b, 3)
                pt_copy(b, 2)
                lay_labels(b)
                q_cols(a, 1)
                ctx_copy(b, 2)
                pt_copy(b, 3)
                kv_cols(a)
                ctx_copy(b, 3)
                x1_cols(b, 0)
                x1_cols(b, 1)

            act.wait_ge(zeroed, 1)
            nc.scalar.activation(gs[:], mg[:, 0, 0:TT], ACT.Exp)
            act.dma_start(Wqn[:], wq.rearrange("(c p) n -> p c n", p=P)).then_inc(d_q, 16)
            x_cols(0)
            for k in range(KT):
                act.wait_ge(WT_ps, k + 1)
                copy(WT[0][:, k], bank[3 + k][:]).then_inc(WT_h, 1)
            lay_adapters(0)
            act.wait_ge(RAT_ps, 1)
            copy(RAT[:].rearrange("p c n -> p (c n)"), OUT[:, 0:KT * EW]).then_inc(RAT_sb, 1)
            act.wait_ge(d_b, 16)
            y_cols(0, 0)
            y_cols(0, 1)
            act.wait_ge(RT_ps, 1)
            copy(RT[:].rearrange("p c n -> p (c n)"), PTB[:, 0:KT * EW]).then_inc(RT_sb, 1)
            q_cols(0, 0)
            q_cols(0, 1)
            kv_cols(0)
            act.wait_ge(C4_ps, 1)
            copy(C4[:], OUT[:, 0:EW]).then_inc(C4_sb, 1)
            act.wait_ge(BT_ps, 1)
            nc.scalar.mul(BT[:].rearrange("q (p k) -> q k p", k=KT),
                          CTX[0:E * R].rearrange("q (k p) -> q k p", k=KT), 4.0).then_inc(BT_sb, 1)
            act.wait_ge(d_o, 16 * NG)
            for h in range(PH):
                copy(Wo[0][:, h], Won[:, h]).then_inc(Wo_h, 1)
            both(1, 0, first=True)
            with act.Fori(1, G - 1) as g:
                both(g + 1, g)
            b = G - 1
            exp(b, 0)
            exp(b, 1)
            pt_copy(b, 0, FR[0])
            exp(b, 2)
            ctx_copy(b, 0, CTX)
            pt_copy(b, 1, FR[1])
            ctx_copy(b, 1, SMALL)
            exp(b, 3)
            lay_labels(b)
            pt_copy(b, 2, FR[0])
            gate_exp(b - 1)
            ctx_copy(b, 2, CTX)
            pt_copy(b, 3, FR[1])
            ctx_copy(b, 3, SMALL)
            mgT_copy(b - 1)
            x1_cols(b, 0, LB)
            x1_cols(b, 1, LB)
            gate_exp(b, 0)
            mgT_copy(b, 0, LB)
            gate_exp(b, 1)
            mgT_copy(b, 1, LB)

        @block.gpsimd
        def _(pool):
            def adapters_rest(g):
                pool.wait_ge(a1_laid, g + 1)
                if not (isinstance(g, int) and g == 0):
                    pool.wait_ge(h_ps, g)
                nc.gpsimd.tensor_tensor(A1[1][:].rearrange("p k s r -> p s k r"), A1n[:],
                                        A1[0][:].bitcast(F32).rearrange("p k s r -> p s k r"), ALU.subtract).then_inc(A1_l, 1)

            def norm(g, j):
                pool.wait_ge(recip, PAIRS * g + j + 1)
                nc.gpsimd.tensor_tensor(ex[:, j], ex[:, j],
                                        ri[:, j, :, None].broadcast_to((P, 2 * NG, T)), ALU.mult).then_inc(normed, 1)

            def shift(g, j):
                pool.wait_ge(maxed, PAIRS * g + j + 1)
                nc.gpsimd.tensor_tensor(sm[:, j % 2], sm[:, j % 2], mx[:, j, :, None].broadcast_to((P, 2 * NG, T)),
                                        ALU.subtract).then_inc(shifted, 1)

            def times_cos(dst, src, n):
                return nc.gpsimd.tensor_tensor(dst, src, CS[:, 0, None, :].broadcast_to((P, n, T)), ALU.mult)

            def q_times_cos(g, h):
                pool.wait_ge(q_sb, 2 * g + h + 1)
                s = slice(2 * h, 2 * h + 2)
                times_cos(qkc[:, s].rearrange("p h (s t) -> p (h s) t", t=T),
                          qk[:, s].rearrange("p h (s t) -> p (h s) t", t=T), 2 * SEQ).then_inc(q_cos, 1)

            def k_times_cos(g):
                pool.wait_ge(kv_sb, 2 * g + 1)
                times_cos(qkc[:, PH].rearrange("p (s t) -> p s t", t=T),
                          qk[:, PH].rearrange("p (s t) -> p s t", t=T), SEQ).then_inc(k_cos, 1)

            def k_sum(g):
                pool.wait_ge(k_sin, g + 1)
                pool.wait_ge(k_cos, g + 1)
                nc.gpsimd.tensor_tensor(kr[:], qkc[:, PH], qks[:, PH], ALU.add).then_inc(k_rope, 1)

            def q_sum(g, h):
                pool.wait_ge(q_sin, 2 * g + h + 1)
                pool.wait_ge(q_cos, 2 * g + h + 1)
                s = slice(2 * h, 2 * h + 2)
                nc.gpsimd.tensor_tensor(qr[:, :, s, :].rearrange("p s h t -> p h s t"),
                                        qkc[:, s].rearrange("p h (s t) -> p h s t", t=T),
                                        qks[:, s].rearrange("p h (s t) -> p h s t", t=T), ALU.add).then_inc(q_rope, 1)

            def k_blocks(g, j):
                if j == 0:
                    pool.wait_ge(k_rope, g + 1)
                for s in (2 * j, 2 * j + 1):
                    i = nc.gpsimd.tensor_tensor(Kbd[:, s], kr[:, None, T * s:T * (s + 1)].broadcast_to((P, NG, T)),
                                                K[:, C_KG:C_KG + NG, None].broadcast_to((P, NG, T)), ALU.mult)
                i.then_inc(kbd_sb, 1)

            def rope(g):
                k_sum(g)
                k_blocks(g, 0)
                q_sum(g, 0)
                q_sum(g, 1)
                for j in range(1, PAIRS):
                    k_blocks(g, j)

            pool.wait_ge(d_ids, 32)
            load_slots(pool, 0, range(POOL_SLOTS), d_slot_pool)
            adapters_rest(0)
            pool.wait_ge(CS_sb, 1)
            q_times_cos(0, 0)
            k_times_cos(0)
            rope(0)
            with pool.Fori(0, G - 1) as g:
                adapters_rest(g + 1)
                norm(g, 0)
                norm(g, 1)
                norm(g, 2)
                norm(g, 3)
                q_times_cos(g + 1, 0)
                q_times_cos(g + 1, 1)
                k_times_cos(g + 1)
                rope(g + 1)
            b = G - 1
            shift(b, 0)
            shift(b, 1)
            norm(b, 0)
            shift(b, 2)
            norm(b, 1)
            shift(b, 3)
            norm(b, 2)
            norm(b, 3)

        @block.vector
        def _(dve):
            V = nc.vector

            def x_rest(g):
                for h in range(2):
                    dve.wait_ge(xT_sb, 2 * g + h + 1)
                    V.tensor_tensor(xT[1][:, 2 * h:2 * h + 2].rearrange("p k t -> p (k t)"), FR[h][:],
                                    xT[0][:, 2 * h:2 * h + 2].bitcast(F32).rearrange("p k t -> p (k t)"),
                                    ALU.subtract).then_inc(xT_l, 1)

            def y_split(g, h):
                for c in (2 * h, 2 * h + 1):
                    dve.wait_ge(y_sb, KT * g + c + 1)
                    V.tensor_copy(yS[0][:, c], yT[:, c]).then_inc(yT_h, 1)
                    dve.wait_ge(yT_h, KT * g + c + 1)
                    V.tensor_tensor(yS[1][:, c], yT[:, c], yS[0][:, c].bitcast(F32), ALU.subtract).then_inc(yT_l, 1)

            def ctx_rest(g, j, src=CTX):
                dve.wait_ge(ctx_sb, PAIRS * g + j + 1)
                V.tensor_tensor(cT[1][:, :, 2 * j:2 * j + 2, :].rearrange("p h s t -> p s h t"),
                                src[:, 0:2 * P].rearrange("p (s h t) -> p s h t", s=2, h=PH),
                                cT[0][:, :, 2 * j:2 * j + 2, :].bitcast(F32).rearrange("p h s t -> p s h t"),
                                ALU.subtract).then_inc(cT_l, 1)

            def adapter_mask(g):
                dve.wait_ge(h_ps, g + 1)
                V.tensor_tensor(hT[:].rearrange("p (s t) -> p s t", t=T), SMALL[:, 0:TOK].rearrange("p (s t) -> p s t", t=T),
                                K[:, C_SLOT:C_SLOT + SEQ, None].broadcast_to((P, SEQ, T)), ALU.mult).then_inc(h_sb, 1)

            def mask_max(g, j):
                dve.wait_ge(sc_ps, PAIRS * g + j + 1)
                V.tensor_tensor(sm[:, j % 2], SC[j % 2][:].rearrange("p (a s) -> p a s", s=T),
                                K[:, None, C_CAUSAL:C_CAUSAL + T].broadcast_to((P, 2 * NG, T)), ALU.add).then_inc(masked, 1)
                dve.wait_ge(masked, PAIRS * g + j + 1)
                V.tensor_reduce(mx[:, j], sm[:, j % 2], AX.X, ALU.max).then_inc(maxed, 1)

            def shift(g, j):
                mask_max(g, j)
                dve.wait_ge(maxed, PAIRS * g + j + 1)
                V.tensor_tensor(sm[:, j % 2], sm[:, j % 2], mx[:, j, :, None].broadcast_to((P, 2 * NG, T)),
                                ALU.subtract).then_inc(shifted, 1)

            def sums(g, j):
                dve.wait_ge(exped, PAIRS * g + j + 1)
                V.tensor_reduce(su[:, j], ex[:, j], AX.X, ALU.add).then_inc(summed, 1)
                dve.wait_ge(summed, PAIRS * g + j + 1)
                V.reciprocal(ri[:, j], su[:, j]).then_inc(recip, 1)

            def times_sin(dst, src, n):
                return V.tensor_tensor(dst, src, CS[:, 1, None, :].broadcast_to((P, n, T)), ALU.mult)

            def k_times_sin(g):
                dve.wait_ge(rotk_ps, g + 1)
                times_sin(qks[:, PH].rearrange("p (s t) -> p s t", t=T),
                          SMALL[:, 0:TOK].rearrange("p (s t) -> p s t", t=T), SEQ).then_inc(k_sin, 1)

            def q_times_sin(g, h):
                dve.wait_ge(rotq_ps, 2 * g + h + 1)
                times_sin(qks[:, 2 * h:2 * h + 2].rearrange("p h (s t) -> p (h s) t", t=T),
                          FR[h][:].rearrange("p (a t) -> p a t", t=T), 2 * SEQ).then_inc(q_sin, 1)

            def v_blocks(g, t):
                dve.wait_ge(vr_ps, TT * g + t + 1)
                for half in range(2):
                    V.tensor_tensor(Vbd[:, half, 4 * t:4 * t + 4].rearrange("p s (g d) -> p s g d", d=HD),
                                    SMALL[:].rearrange("p (s g d) -> p s g d", s=4, d=HD),
                                    K[:, None, C_VG + NG * half:C_VG + NG * (half + 1), None].broadcast_to((P, 4, NG, HD)),
                                    ALU.mult).then_inc(vbd_sb, 1)

            def residual(g, t, tb=TB, dst=None):
                dve.wait_ge(wo_ps, TT * g + t + 1)
                dve.wait_ge(d_xres, 16 * (TT * g + TT))
                if not (isinstance(g, int) and g in (0, G - 1)):
                    dve.wait_ge(d_out, 16 * TT * g)
                V.tensor_tensor((dst or x1)[:, t], tb[t][:], xres[:, t], ALU.add).then_inc(x1_sb, 1)

            def label_mask(g, t, tb=TB):
                dve.wait_ge(low_ps, TT * g + t + 1)
                V.tensor_tensor(lT[:, t].rearrange("p (s t) -> p s t", t=T), tb[t][:, 0:P].rearrange("p (s t) -> p s t", t=T),
                                K[:, C_LABEL:C_LABEL + 4, None].broadcast_to((P, 4, T)), ALU.mult).then_inc(low_sb, 1)

            def gates(g, one=None, tb=TB):
                tiles = range(TT) if one is None else (one,)
                n, ts, nt = (0, slice(0, TT), TT) if one is None else (one, slice(one, one + 1), 1)

                def step(i, ins):
                    ins.then_inc(g_step, 1)
                    dve.wait_ge(g_step, 10 * (g + n) + i)

                for t in tiles:
                    dve.wait_ge(mid_ps, TT * g + t + 1)
                    V.tensor_copy(mid[:, t], tb[t][:, 0:EW]).then_inc(mid_sb, 1)
                dve.wait_ge(mid_sb, TT * g + tiles[-1] + 1)
                lg = mid[:, ts, E * R:EW]
                of_j, of_e = lg[:, :, None, :].broadcast_to((P, nt, E, E)), lg[:, :, :, None].broadcast_to((P, nt, E, E))
                step(1, V.tensor_reduce(m1[:, ts], lg, AX.X, ALU.max))
                step(2, V.tensor_tensor(lm[:, ts], lg, m1[:, ts, None].broadcast_to((P, nt, E)), ALU.subtract))
                step(3, V.tensor_tensor(eq[:, ts], of_j, of_e, ALU.is_equal))
                step(4, V.tensor_tensor(eq[:, ts], eq[:, ts], K[:, None, C_TRI:C_TRI + E * E].rearrange("p a (e j) -> p a e j", e=E)
                                        .broadcast_to((P, nt, E, E)), ALU.mult))
                step(5, V.tensor_tensor(gt[:, ts], of_j, of_e, ALU.is_gt))
                step(6, V.tensor_tensor(gt[:, ts], gt[:, ts], eq[:, ts], ALU.add))
                step(7, V.tensor_reduce(rk[:, ts], gt[:, ts], AX.X, ALU.add))
                dve.wait_ge(g_exp, g + n + 1)
                step(8, V.scalar_tensor_tensor(out=gw[:, ts], in0=rk[:, ts], scalar=1.5, in1=le[:, ts], op0=ALU.is_lt, op1=ALU.mult))
                step(9, V.tensor_reduce(gs[:, ts], gw[:, ts], AX.X, ALU.add))
                step(10, V.reciprocal(gr[:, ts], gs[:, ts]))
                V.tensor_tensor(gate[:, ts], gw[:, ts], gr[:, ts, None].broadcast_to((P, nt, E)), ALU.mult).then_inc(gated, 1)
                dve.wait_ge(gated, g + n + 1)
                for t in tiles:
                    V.tensor_tensor(mg[:, t, 0:E * R].rearrange("p (e r) -> p e r", e=E), mid[:, t, 0:E * R].rearrange("p (e r) -> p e r", e=E),
                                    gate[:, t, :, None].broadcast_to((P, E, R)), ALU.mult).then_inc(g_mid, 1)

            def finish(g, order=(1, 0), tb=TB, dst=None):
                for n, t in enumerate(order):
                    dve.wait_ge(dl_ps, TT * g + n + 1)
                    V.tensor_tensor((dst or x1)[:, t], tb[t][:], (dst or x1)[:, t], ALU.add).then_inc(fin_sb, 1)

            def both(a, b, first=False):
                x_rest(a)
                shift(b, 0)
                shift(b, 1)
                if first:
                    for h in range(PH):
                        dve.wait_ge(Wo_h, h + 1)
                        V.tensor_tensor(Wo[1][:, h], Won[:, h], Wo[0][:, h].bitcast(F32), ALU.subtract).then_inc(Wo_l, 1)
                adapter_mask(a)
                if not first:
                    gates(b - 1)
                sums(b, 0)
                y_split(a, 0)
                sums(b, 1)
                if not first:
                    finish(b - 1)
                y_split(a, 1)
                shift(b, 2)
                ctx_rest(b, 0)
                sums(b, 2)
                shift(b, 3)
                ctx_rest(b, 1)
                sums(b, 3)
                ctx_rest(b, 2)
                ctx_rest(b, 3)
                k_times_sin(a)
                residual(b, 0)
                q_times_sin(a, 0)
                q_times_sin(a, 1)
                residual(b, 1)
                v_blocks(a, 0)
                label_mask(b, 0)
                v_blocks(a, 1)
                label_mask(b, 1)

            V.memset(mg[:], 0.0).then_inc(zeroed, 1)
            x_rest(0)
            for k in range(KT):
                dve.wait_ge(WT_h, k + 1)
                V.tensor_tensor(WT[1][:, k], bank[3 + k][:], WT[0][:, k].bitcast(F32), ALU.subtract).then_inc(WT_l, 1)
            dve.wait_ge(d_K, 16)
            V.tensor_copy(spread[:], ident.rearrange("p (s t) -> p s t", s=4)[:, :, None, :].broadcast_to((P, 4, 4, T))).then_inc(spread_laid, 1)
            dve.wait_ge(d_q, 16)
            for c in range(KT):
                wide = Wqn[:, c].rearrange("p (g h d) -> p h g d", g=NG, h=PH)
                V.tensor_copy(Wq[0][:, c].rearrange("p h (g d) -> p h g d", g=NG), wide).then_inc(Wq_h, 1)
                dve.wait_ge(Wq_h, c + 1)
                V.tensor_tensor(Wq[1][:, c].rearrange("p h (g d) -> p h g d", g=NG), wide,
                                Wq[0][:, c].bitcast(F32).rearrange("p h (g d) -> p h g d", g=NG), ALU.subtract).then_inc(wq_laid, 1)
            adapter_mask(0)
            dve.wait_ge(d_cs, 32)
            V.tensor_copy(cs8[:], cs[:, :, None, :].broadcast_to((T, 2, NG, HD))).then_inc(cs_laid, 1)
            y_split(0, 0)
            y_split(0, 1)
            dve.wait_ge(CS_ps, 1)
            V.tensor_copy(CS[:].rearrange("p a t -> p (a t)"), bank[3][:, 0:2 * T]).then_inc(CS_sb, 1)
            dve.wait_ge(d_k, 16)
            V.tensor_copy(Wk[0][:], Wkn[:]).then_inc(Wk_h, 1)
            dve.wait_ge(Wk_h, 1)
            V.tensor_tensor(Wk[1][:], Wkn[:], Wk[0][:].bitcast(F32), ALU.subtract).then_inc(Wk_l, 1)
            dve.wait_ge(d_bw, 16)
            V.tensor_copy(Bw4[:], Bw[:, :, None, :].broadcast_to((P, KT, 4, R2))).then_inc(bw_laid, 1)
            dve.wait_ge(d_bf, 16)
            V.tensor_copy(Bk[:], Bf[:].rearrange("p e k r -> p k e r")).then_inc(bf_laid, 1)
            dve.wait_ge(q_sb, 2)
            V.tensor_tensor(qkc[:, 2:4].rearrange("p h (s t) -> p (h s) t", t=T), qk[:, 2:4].rearrange("p h (s t) -> p (h s) t", t=T),
                            CS[:, 0, None, :].broadcast_to((P, 2 * SEQ, T)), ALU.mult).then_inc(q_cos, 1)
            k_times_sin(0)
            q_times_sin(0, 0)
            q_times_sin(0, 1)
            v_blocks(0, 0)
            v_blocks(0, 1)
            both(1, 0, first=True)
            with dve.Fori(1, G - 1) as g:
                both(g + 1, g)
            b = G - 1
            mask_max(b, 0)
            mask_max(b, 1)
            sums(b, 0)
            mask_max(b, 2)
            sums(b, 1)
            mask_max(b, 3)
            ctx_rest(b, 0, CTX)
            sums(b, 2)
            ctx_rest(b, 1, SMALL)
            sums(b, 3)
            gates(b - 1)
            ctx_rest(b, 2, CTX)
            residual(b, 0, LB, xres)
            ctx_rest(b, 3, SMALL)
            finish(b - 1)
            label_mask(b, 0, LB)
            residual(b, 1, LB, xres)
            gates(b, 0, LB)
            label_mask(b, 1, LB)
            gates(b, 1, LB)
            finish(b, (0, 1), LB, xres)

        @block.tensor
        def _(pe):
            def mm(dst, lhsT, rhs, start, stop):
                return nc.tensor.matmul(dst, lhsT, rhs, start=start, stop=stop)

            def mm3(dst, lhsT, rhs, start, stop):
                mm(dst, lhsT[0], rhs[0], start, False)
                mm(dst, lhsT[0], rhs[1], False, False)
                return mm(dst, lhsT[1], rhs[0], False, stop)

            def tr(dst, src, n=P):
                return nc.tensor.transpose(dst, src, ident[0:n, 0:n])

            def x_transposes(g):
                pe.wait_ge(d_x, 16 * (TT * g + TT))
                for h in range(2):
                    for k in (2 * h, 2 * h + 1):
                        for t in range(TT):
                            c = (k % 2) * TOK + t * P
                            i = tr(FR[h][:, c:c + P], xin[:, t, k:D:KT])
                    i.then_inc(xT_ps, 1)

            def adapter_in(g):
                pe.wait_ge(A1_l, g + 1)
                for k in range(KT):
                    i = mm3(SMALL[:, 0:TOK], [w[:, k].rearrange("p s r -> p (s r)") for w in A1],
                            [z[:, k] for z in xT], k == 0, k == KT - 1)
                i.then_inc(h_ps, 1)

            def y_base(g, h):
                for c in (2 * h, 2 * h + 1):
                    dst = FR[h][:, (c % 2) * TOK:(c % 2 + 1) * TOK]
                    for k in range(KT):
                        w, z = [w[:, k, P * c:P * (c + 1)] for w in WT], [z[:, k] for z in xT]
                        for n, (u, r) in enumerate(((0, 0), (0, 1), (1, 0))):
                            if isinstance(g, int) and g == 0 and c == 0 and n == 0:
                                pe.wait_ge(WT_l, k + 1)
                            nc.tensor.matmul(dst, w[u], z[r], start=(c % 2 == 0 and k == 0 and n == 0), stop=False,
                                             skip_group_check=True)

            def y_adapter(g, h):
                if h == 0:
                    pe.wait_ge(h_sb, g + 1)
                for c in (2 * h, 2 * h + 1):
                    dst = FR[h][:, (c % 2) * TOK:(c % 2 + 1) * TOK]
                    i = nc.tensor.matmul(dst, B1[:, P * c:P * (c + 1)], hT[:], start=False, stop=True, skip_group_check=True)
                i.then_inc(y_ps, 1)

            def y_tiles(g, h):
                y_base(g, h)
                y_adapter(g, h)

            def q_tiles(g, h):
                if h == 0:
                    pe.wait_ge(yT_l, KT * (g + 1))
                for q in (2 * h, 2 * h + 1):
                    dst = FR[h][:, (q % 2) * TOK:(q % 2 + 1) * TOK]
                    for c in range(KT):
                        i = mm3(dst, [w[:, c, q] for w in Wq], [z[:, c] for z in yS], c == 0, c == KT - 1)
                i.then_inc(q_ps, 1)

            def kv_tiles(g):
                for c in range(KT):
                    mm3(SMALL[:, 0:TOK], [w[:, c] for w in Wk], [z[:, c] for z in yS], c == 0, c == KT - 1)
                for t in range(TT):
                    for c in range(KT):
                        i = mm(SMALL[:, TOK + P * t:TOK + P * (t + 1)], yT[:, c, P * t:P * (t + 1)], Wv[:, c],
                               c == 0, c == KT - 1)
                i.then_inc(kv_ps, 1)

            def rotate_k(g):
                pe.wait_ge(kv_sb, 2 * g + 2)
                mm(SMALL[:, 0:TOK], rot, qk[:, PH], True, True).then_inc(rotk_ps, 1)

            def rotate_q(g):
                for h in range(2):
                    pe.wait_ge(q_sb, 2 * g + h + 1)
                    mm(FR[h][:], rot, qk[:, 2 * h:2 * h + 2].rearrange("p h t -> p (h t)"), True, True).then_inc(rotq_ps, 1)

            def v_spread(g, t):
                if t == 0:
                    pe.wait_ge(k_sin, g + 1)
                else:
                    pe.wait_ge(vbd_sb, 2 * TT * g + 2)
                for s in range(4):
                    i = mm(SMALL[:, P * s:P * (s + 1)],
                           spread[:, s].rearrange("p a t -> p (a t)"), v[:, t], True, True)
                i.then_inc(vr_ps, 1)

            def scores(g, j):
                if j < 2:
                    pe.wait_ge(q_rope, 2 * g + 2)
                    if not (isinstance(g, int) and g == 0):
                        pe.wait_ge(masked, PAIRS * g - 2 + j + 1)
                else:
                    pe.wait_ge(masked, PAIRS * g + j - 1)
                pe.wait_ge(kbd_sb, PAIRS * g + j + 1)
                for s in range(2):
                    i = mm(SC[j % 2][:, 2 * P * s:2 * P * (s + 1)], qr[:, 2 * j + s].rearrange("p h t -> p (h t)"),
                           Kbd[:, 2 * j + s].rearrange("p g t -> p (g t)"), True, True)
                i.then_inc(sc_ps, 1)

            def p_transposes(g, j, dst=PTB, banks=1):
                pe.wait_ge(normed, PAIRS * g + j + 1)
                if j >= banks:
                    pe.wait_ge(pt_sb, PAIRS * g + j - banks + 1)
                for s in range(2):
                    for half in range(2):
                        c = (2 * s + half) * P
                        i = tr(dst[:, c:c + P], ex[:, j].rearrange("p a t -> p (a t)")[:, c:c + P])
                i.then_inc(pt_ps, 1)

            def context(g, j, dst=CTX, banks=1):
                pe.wait_ge(pt_sb, PAIRS * g + j + 1)
                if j == 0:
                    pe.wait_ge(vbd_sb, 2 * TT * (g + 1))
                if j >= banks:
                    pe.wait_ge(cT_l, PAIRS * g + j - banks + 1)
                for s in range(2):
                    for half in range(2):
                        i = mm(dst[:, P * s:P * (s + 1)], Vbd[:, half, 2 * j + s], PT[:, j % 2, s, half], half == 0, half == 1)
                i.then_inc(ctx_ps, 1)

            def project(g, t, tb=TB):
                pe.wait_ge(cT_l, PAIRS * g + 2 * (t + 1))
                if isinstance(g, int) and g == 0 and t == 0:
                    pe.wait_ge(Wo_l, PH)
                for h in range(PH):
                    i = mm3(tb[t][:], [c[:, h, 4 * t:4 * t + 4].rearrange("p s t -> p (s t)") for c in cT],
                            [w[:, h] for w in Wo], h == 0, h == PH - 1)
                i.then_inc(wo_ps, 1)

            def x1_transposes(g, t, tb=TB, src=None):
                pe.wait_ge(x1_sb, TT * g + t + 1)
                for k in range(KT):
                    i = tr(tb[t][:, P * k:P * (k + 1)], (src or x1)[:, t, k:D:KT])
                i.then_inc(x1T_ps, 1)

            def label_in(g, t, tb=TB):
                pe.wait_ge(x1T_sb, TT * g + t + 1)
                pe.wait_ge(a2_laid, g + 1)
                for k in range(KT):
                    i = mm(tb[t][:, 0:P], A2[:, k, 4 * t:4 * t + 4].rearrange("p s r -> p (s r)"), x1T[:, t, k], k == 0, k == KT - 1)
                i.then_inc(low_ps, 1)

            def mid_logits(g, t, tb=TB):
                pe.wait_ge(low_sb, TT * g + t + 1)
                for k in range(KT):
                    mm(tb[t][:, 0:EW], x1T[:, t, k], RT[:, k], k == 0, False)
                mm(tb[t][:, 0:EW], lT[:, t], C4[:], False, True).then_inc(mid_ps, 1)

            def mid_transpose(g, t, tb=TB):
                pe.wait_ge(g_mid, TT * g + t + 1)
                tr(tb[t][:, 0:P], mg[:, t]).then_inc(mgT_ps, 1)

            def delta(g, t, copied=TT, tb=TB):
                pe.wait_ge(mgT_sb, TT * g + copied)
                mm(tb[t][:], mgT[:, t], BT[:], True, True).then_inc(dl_ps, 1)

            def both(a, b, first=False):
                x_transposes(a)
                if first:
                    scores(b, 0)
                scores(b, 1)
                pe.wait_ge(xT_l, 2 * a + 2)
                if first:
                    y_base(a, 0)
                    adapter_in(a)
                    y_base(a, 1)
                    y_adapter(a, 0)
                else:
                    adapter_in(a)
                    y_tiles(a, 0)
                    y_base(a, 1)
                    mid_transpose(b - 1, 0)
                    mid_transpose(b - 1, 1)
                y_adapter(a, 1)
                if not first:
                    delta(b - 1, 1)
                    delta(b - 1, 0)
                scores(b, 2)
                if not first:
                    pe.wait_ge(fin_sb, TT * (b - 1) + 1)
                p_transposes(b, 0)
                scores(b, 3)
                context(b, 0)
                p_transposes(b, 1)
                q_tiles(a, 0)
                context(b, 1)
                p_transposes(b, 2)
                q_tiles(a, 1)
                context(b, 2)
                p_transposes(b, 3)
                kv_tiles(a)
                context(b, 3)
                rotate_k(a)
                if not first:
                    pe.wait_ge(fin_sb, TT * b)
                project(b, 0)
                rotate_q(a)
                project(b, 1)
                x1_transposes(b, 0)
                v_spread(a, 0)
                x1_transposes(b, 1)
                label_in(b, 0)
                scores(a, 0)
                v_spread(a, 1)
                label_in(b, 1)
                mid_logits(b, 0)
                mid_logits(b, 1)

            pe.wait_ge(d_K, 16)
            x_transposes(0)
            for c in range(KT):
                pe.wait_ge(d_W[c], 16)
                for k in range(KT):
                    i = tr(bank[3 + k][:, P * c:P * (c + 1)], Wn[:, c, k:D:KT])
                    if c == KT - 1:
                        i.then_inc(WT_ps, 1)
            pe.wait_ge(xT_l, 2)
            y_base(0, 0)
            y_base(0, 1)
            pe.wait_ge(d_ra, 32)
            for c in range(KT):
                i = tr(OUT[:, EW * c:EW * (c + 1)], RA[:, P * c:P * (c + 1)], EW)
            i.then_inc(RAT_ps, 1)
            adapter_in(0)
            y_adapter(0, 0)
            y_adapter(0, 1)
            pe.wait_ge(cs_laid, 1)
            for a in range(2):
                i = mm(bank[3][:, T * a:T * (a + 1)], cs8[:, a].rearrange("t g d -> t (g d)"), ident[0:T, 0:T], True, True)
            i.then_inc(CS_ps, 1)
            pe.wait_ge(RAT_sb, 1)
            pe.wait_ge(d_w2, 16)
            for k in range(KT):
                for c in range(KT):
                    i = mm(PTB[:, EW * k:EW * (k + 1)], W2[:, c, k:D:KT], RAT[:, c], c == 0, c == KT - 1)
            i.then_inc(RT_ps, 1)
            pe.wait_ge(wq_laid, KT)
            q_tiles(0, 0)
            q_tiles(0, 1)
            pe.wait_ge(Wk_l, 1)
            pe.wait_ge(d_v, 16)
            kv_tiles(0)
            pe.wait_ge(bw_laid, 1)
            for c in range(KT):
                i = mm(OUT[:, 0:EW], Bw4[:, c].rearrange("p a r -> p (a r)"), RAT[:, c], c == 0, c == KT - 1)
            i.then_inc(C4_ps, 1)
            rotate_k(0)
            rotate_q(0)
            pe.wait_ge(spread_laid, 1)
            v_spread(0, 0)
            pe.wait_ge(bf_laid, 1)
            for c in range(KT):
                i = tr(CTX[0:E * R, P * c:P * (c + 1)], Bk[:, c].rearrange("p e r -> p (e r)"))
            i.then_inc(BT_ps, 1)
            v_spread(0, 1)
            pe.wait_ge(RT_sb, 1)
            pe.wait_ge(C4_sb, 1)
            pe.wait_ge(BT_sb, 1)
            both(1, 0, first=True)
            with pe.Fori(1, G - 1) as g:
                both(g + 1, g)
            b = G - 1
            scores(b, 1)
            scores(b, 2)
            scores(b, 3)
            p_transposes(b, 0, FR[0], 2)
            context(b, 0, CTX, 2)
            p_transposes(b, 1, FR[1], 2)
            context(b, 1, SMALL, 2)
            p_transposes(b, 2, FR[0], 2)
            project(b, 0, LB)
            context(b, 2, CTX, 2)
            p_transposes(b, 3, FR[1], 2)
            context(b, 3, SMALL, 2)
            mid_transpose(b - 1, 0)
            mid_transpose(b - 1, 1)
            x1_transposes(b, 0, LB, xres)
            delta(b - 1, 1)
            delta(b - 1, 0)
            label_in(b, 0, LB)
            project(b, 1, LB)
            mid_logits(b, 0, LB)
            x1_transposes(b, 1, LB, xres)
            label_in(b, 1, LB)
            mid_transpose(b, 0, LB)
            mid_logits(b, 1, LB)
            delta(b, 0, 1, LB)
            mid_transpose(b, 1, LB)
            delta(b, 1, TT, LB)


_INS = ["x", "itok_B_0_23", "itok_B_0_2", "L0_cond_W", "L0_cond_b", "L0_cond_lora_As", "L0_cond_lora_Bs",
        "L0_attn_Wq", "L0_attn_Wk", "L0_attn_Wv", "L0_attn_Wo", "L0_attn_cos", "L0_attn_sin",
        "L0_cond2_W", "L0_cond2_lora_A", "L0_cond2_lora_B_w", "L0_ffn_router_w", "L0_ffn_A", "L0_ffn_B"]


def kernel(**inputs):
    import concourse.bacc as bacc
    from concourse.bass_utils import run_bass_kernel_spmd

    nc = bacc.Bacc("TRN2", target_bir_lowering=False, num_devices=1)
    arrays, args = {}, []
    for name in _INS:
        a = np.ascontiguousarray(inputs[name])
        arrays[name] = a
        args.append(nc.dram_tensor(name, a.shape, mybir.dt.from_np(a.dtype), kind="ExternalInput").ap())
    arrays["constants"] = shape_constants()
    args.append(nc.dram_tensor("constants", (P, C_N), F32, kind="ExternalInput").ap())
    args.append(nc.dram_tensor("out", (B, T, D), F32, kind="ExternalOutput").ap())
    program(nc, *args)
    r = run_bass_kernel_spmd(nc, [arrays], core_ids=[0])
    return r.results[0]["out"]
```

```python
from contextlib import ExitStack

import numpy as np
import concourse.bass as bass
from concourse import mybir

F32 = mybir.dt.float32
F32R = mybir.dt.float32r
I32 = mybir.dt.int32
ALU = mybir.AluOpType
ACT = mybir.ActivationFunctionType
AX = mybir.AxisListType

P = 128
B, T, D = 32, 32, 512
KT = D // P
G = 4
SEQ = B // G
TOK = SEQ * T
TT = TOK // P
HD, NG, PH = 16, 8, 4
R1, R2 = 16, 32
SLOTS, LABELS = 32, 5
E, R = 4, 16
EW = E * R + E
PAIRS = SEQ // 2
NEG = -3.0e38
STEPS = 9
POOL_SLOTS = 3

C_ID, C_ROT, C_CAUSAL, C_KG, C_SLOT, C_LABEL, C_VG, C_TRI, C_N = 0, 128, 256, 288, 296, 304, 308, 340, 372


def shape_constants():
    c = np.zeros((P, C_N), np.float32)
    p = np.arange(P)
    c[:, C_ID:C_ID + P] = np.eye(P)
    for m in range(P):
        if m % HD < HD // 2:
            c[m + HD // 2, C_ROT + m] = -1
        else:
            c[m - HD // 2, C_ROT + m] = 1
    c[:, C_CAUSAL:C_CAUSAL + T] = np.where(np.arange(T)[None] <= (p % T)[:, None], 0, NEG)
    c[:, C_KG:C_KG + NG] = (p // HD)[:, None] == np.arange(NG)
    c[:, C_SLOT:C_SLOT + SEQ] = 2.0 * ((p // R1)[:, None] == np.arange(SEQ))
    c[:, C_LABEL:C_LABEL + 4] = 0.5 * ((p // R2)[:, None] == np.arange(4))
    for half in range(2):
        c[:, C_VG + 2 * NG * half:C_VG + 2 * NG * (half + 1)] = (p // T + 4 * half)[:, None] == np.arange(2 * NG) % NG
    j_before_e = np.arange(E)[None, :] < np.arange(E)[:, None]
    c[:, C_TRI:C_TRI + 2 * E * E] = np.stack([j_before_e, ~j_before_e], 1).reshape(-1)
    return c


def program(nc, x, slot_ids, label_ids, cW, cb, lA, lB, wq, wk, wv, wo, cos, sin, w2, a2, bw, rw, fA, fB, consts, out):
    ctx = ExitStack()
    with ctx:
        def sb(name, shape, dt=F32):
            return ctx.enter_context(nc.sbuf_tensor(name, shape, dt))

        def sem(name):
            return ctx.enter_context(nc.semaphore(name))

        K = sb("K", [P, C_N])
        ids = sb("ids", [1, 2, B], I32)
        Wn = sb("Wn", [P, KT, D])
        W2 = Wn
        WT = [sb(f"WT{i}", [P, KT, D], F32R) for i in "hl"]
        bias = sb("bias", [P, KT])
        Wqn = sb("Wqn", [P, KT, D])
        Wq = [sb(f"Wq{i}", [P, KT, PH, P], F32R) for i in "hl"]
        Wkn = sb("Wkn", [P, KT, P])
        Wk = [sb(f"Wk{i}", [P, KT, P], F32R) for i in "hl"]
        Wv = sb("Wv", [P, KT, P])
        Won = Wqn
        Wo = [sb(f"Wo{i}", [P, PH, D], F32R) for i in "hl"]
        Bw = sb("Bw", [P, KT, R2])
        RAT = sb("RAT", [P, KT, EW])
        RT = sb("RT", [P, KT, EW])
        C4 = sb("C4", [P, EW])
        BT = [sb("BTh", [P, D], F32R),
              sb("BTl", [E * R, D], F32R)]
        cs = sb("cs", [T, 2, HD])
        cs8 = sb("cs8", [T, 2, NG, HD])
        spread = sb("spread", [P, 4, 4, T], F32R)
        CS = sb("CS", [P, 2, T])
        xin = sb("xin", [P, TT, D])
        A1n = sb("A1n", [P, SEQ, KT, R1])
        A1 = [sb(f"A1{i}", [P, KT, SEQ, R1], F32R) for i in "hl"]
        B1 = sb("B1", [P, D])
        xT = [sb(f"xT{i}", [P, KT, TOK], F32R) for i in "hl"]
        hT = sb("hT", [P, TOK])
        yT = sb("yT", [P, KT, TOK])
        yS = [sb(f"yT{i}", [P, KT, TOK], F32R) for i in "hl"]
        qh = sb("qh", [P, PH, TOK], F32R)
        kT = sb("kT", [P, TOK])
        qkc = sb("qkc", [P, PH + 1, TOK])
        ql = xT[1]
        qks = sb("qks", [P, PH + 1, TOK])
        rot2 = sb("rot2", [P, P], F32R)
        qr = sb("qr", [P, SEQ, PH, T])
        kr = sb("kr", [P, TOK])
        Kbd = sb("Kbd", [P, SEQ, NG, T])
        v = [sb(f"v{i}", [P, TT, P], F32R) for i in "hl"]
        Vbd = sb("Vbd", [P, 2, SEQ, P])
        sm = sb("sm", [P, 2, 2 * NG, T])
        mx = sb("mx", [P, PAIRS, 2 * NG])
        ex = sb("ex", [P, PAIRS, 2 * NG, T])
        room = ex[:].rearrange("p j a b -> p (j a b)")
        Bk = room[:, 0:KT * 2 * E * R].rearrange("p (k i n) -> p k i n", k=KT, i=2)
        Bw4 = room[:, KT * 2 * E * R:][:, 0:KT * 4 * R2].rearrange("p (k i n) -> p k i n", k=KT, i=4)
        Bf = room[:, KT * (2 * E * R + 4 * R2):][:, 0:E * KT * R].rearrange("p (e k r) -> p e k r", e=E, k=KT)
        RA = room[0:EW, KT * (2 * E * R + 4 * R2) + E * KT * R:][:, 0:D]
        su = sb("su", [P, PAIRS, 2 * NG])
        ri = sb("ri", [P, PAIRS, 2 * NG])
        PT = sb("PT", [P, 2, 2, 2, P])
        cT = [sb(f"cT{i}", [P, PH, SEQ, T], F32R) for i in "hl"]
        xres = sb("xres", [P, TT, D])
        x1 = sb("x1", [P, TT, D])
        x1T = sb("x1T", [P, TT, KT, P])
        A2n = sb("A2n", [P, SEQ, KT, R2])
        A2 = sb("A2", [P, KT, SEQ, R2])
        lT = sb("lT", [P, TT, P])
        mid = sb("mid", [P, TT, EW])
        m1 = sb("m1", [P, TT])
        lm = sb("lm", [P, TT, E])
        above = sb("above", [P, TT, E, 2, E])
        rk = sb("rk", [P, TT, E])
        le = sb("le", [P, TT, E])
        gw = sb("gw", [P, TT, E])
        gs = sb("gs", [P, TT])
        gr = sb("gr", [P, TT])
        mg = sb("mg", [P, TT, 2, E * R])
        mgT = sb("mgT", [P, TT, P], F32R)

        bank = [ctx.enter_context(nc.psum_tensor(f"bank{i}", [P, 512], F32)) for i in range(8)]
        FR, SMALL, SC, PTB, CTX, OUT = bank[0:2], bank[2], bank[3:5], bank[5], bank[6], bank[7]
        TB = [OUT, PTB]
        LB = SC

        d_ids, d_K, d_cs, d_b, d_q, d_k, d_v, d_o, d_w2, d_bw, d_ra, d_bf = map(
            sem, "d_ids d_K d_cs d_b d_q d_k d_v d_o d_w2 d_bw d_ra d_bf".split())
        d_x, d_slot, d_xres, d_a2, d_out = map(sem, "d_x d_slot d_xres d_a2 d_out".split())
        d_W = [sem(f"d_W{c}") for c in range(KT)]
        d_slot_pool = sem("d_slot_pool")
        WT_ps, RAT_ps, RAT_sb, CS_ps, CS_sb, RT_ps, RT_sb, C4_ps, C4_sb, BT_ps, BT_h, BT_l, zeroed = map(
            sem, "WT_ps RAT_ps RAT_sb CS_ps CS_sb RT_ps RT_sb C4_ps C4_sb BT_ps BT_h BT_l zeroed".split())
        v_l, WT_h, WT_l, Wq_h, Wk_h, Wk_l, Wo_h, Wo_l, A1_l, xT_l, yT_h, yT_l, cT_l = map(
            sem, "v_l WT_h WT_l Wq_h Wk_h Wk_l Wo_h Wo_l A1_l xT_l yT_h yT_l cT_l".split())
        cs_laid, exact_laid, wq_laid, bw_laid, bf_laid, a1_laid, a2_laid = map(
            sem, "cs_laid exact_laid wq_laid bw_laid bf_laid a1_laid a2_laid".split())
        xT_ps, xT_sb, h_ps, h_sb, y_ps, y_sb, q_ps, q_sb, kv_ps, kv_sb = map(
            sem, "xT_ps xT_sb h_ps h_sb y_ps y_sb q_ps q_sb kv_ps kv_sb".split())
        q_l, rotk_ps, rotq_ps, k_sin, q_sin, k_cos, q_cos, k_rope, q_rope, kbd_sb, vr_ps, vbd_sb = map(
            sem, "q_l rotk_ps rotq_ps k_sin q_sin k_cos q_cos k_rope q_rope kbd_sb vr_ps vbd_sb".split())
        sc_ps, masked, maxed, shifted, exped, summed, recip, normed, pt_ps, pt_sb, ctx_ps, ctx_sb = map(
            sem, "sc_ps masked maxed shifted exped summed recip normed pt_ps pt_sb ctx_ps ctx_sb".split())
        wo_ps, x1_sb, x1T_ps, x1T_sb, low_ps, low_sb, mid_ps, mid_sb = map(
            sem, "wo_ps x1_sb x1T_ps x1T_sb low_ps low_sb mid_ps mid_sb".split())
        g_step, g_exp, g_mid, mgT_ps, mgT_h, mgT_l, dl_ps, fin_sb = map(
            sem, "g_step g_exp g_mid mgT_ps mgT_h mgT_l dl_ps fin_sb".split())

        ident = K[:, C_ID:C_ID + P]
        rot = K[:, C_ROT:C_ROT + P]

        def load_slots(eng, g, seqs=range(SEQ), arrived=d_slot):
            for s in seqs:
                slot = eng.value_load(ids[0:1, 0, bass.ds(g * SEQ + s, 1)], min_val=0, max_val=SLOTS - 1)
                eng.dma_start(A1n[:, s].rearrange("p k r -> p (k r)"),
                              lA[bass.ds(slot, 1)].rearrange("a (p k) r -> p (a k r)", k=KT)).then_inc(arrived, 16)
                eng.dma_start(B1[R1 * s:R1 * (s + 1), :],
                              lB[bass.ds(slot, 1)].rearrange("a r o -> (a r) o")).then_inc(arrived, 16)

        block = ctx.enter_context(nc.Block())

        @block.sync
        def _(sp):
            xf = x.rearrange("(g t s) u d -> g t (s u) d", g=G, t=TT)
            of = out.rearrange("(g t s) u d -> g t (s u) d", g=G, t=TT)

            def load_x(g):
                for t in range(TT):
                    sp.dma_start(xin[:, t, :], xf[bass.ds(g, 1), t].rearrange("a p d -> p (a d)")).then_inc(d_x, 16)

            def load_labels(g):
                for s in range(SEQ):
                    label = sp.value_load(ids[0:1, 1, bass.ds(g * SEQ + s, 1)], min_val=0, max_val=LABELS - 1)
                    sp.dma_start(A2n[:, s].rearrange("p k r -> p (k r)"),
                                 a2[bass.ds(label, 1)].rearrange("a (p k) r -> p (a k r)", k=KT)).then_inc(d_a2, 16)

            def load_xres(g):
                for t in range(TT):
                    sp.dma_start(xres[:, t, :], xf[bass.ds(g, 1), t].rearrange("a p d -> p (a d)")).then_inc(d_xres, 16)

            def front_loads(g):
                sp.wait_ge(xT_ps, 2 * g)
                load_x(g)
                sp.wait_ge(A1_l, g)
                sp.wait_ge(y_ps, 2 * g)
                load_slots(sp, g)

            def back_loads(g):
                sp.wait_ge(x1_sb, TT * g)
                load_xres(g)
                sp.wait_ge(a2_laid, g)
                load_labels(g)

            def store(g):
                sp.wait_ge(fin_sb, TT * (g + 1))
                for t in range(TT):
                    sp.dma_start(of[bass.ds(g, 1), t].rearrange("a p d -> p (a d)"), x1[:, t, :]).then_inc(d_out, 16)

            load_x(0)
            sp.dma_start(ids[:, 0], slot_ids.rearrange("(a b) -> a b", a=1)).then_inc(d_ids, 16)
            sp.dma_start(ids[:, 1], label_ids.rearrange("(a b) -> a b", a=1)).then_inc(d_ids, 16)
            sp.wait_ge(d_ids, 32)
            load_slots(sp, 0, range(POOL_SLOTS, SEQ))
            sp.dma_start(bias[:], cb.rearrange("(c p) -> p c", p=P), allow_slow_non_contiguous=True).then_inc(d_b, 16)
            sp.dma_start(RA[0:E * R], fA.rearrange("e r d -> (e r) d")).then_inc(d_ra, 16)
            sp.dma_start(RA[E * R:EW], rw).then_inc(d_ra, 16)
            sp.dma_start(cs[:, 0], cos[0:T, :]).then_inc(d_cs, 16)
            sp.dma_start(cs[:, 1], sin[0:T, :]).then_inc(d_cs, 16)
            sp.wait_ge(WT_ps, KT)
            sp.dma_start(W2[:], w2.rearrange("(c p) i -> p c i", p=P)).then_inc(d_w2, 16)
            sp.dma_start(Wkn[:], wk.rearrange("(c p) n -> p c n", p=P)).then_inc(d_k, 16)
            sp.dma_start(Wv[:], wv.rearrange("(c p) n -> p c n", p=P)).then_inc(d_v, 16)
            sp.dma_start(Bw[:], bw.rearrange("(c p) r -> p c r", p=P)).then_inc(d_bw, 16)
            sp.dma_start(Bf.rearrange("p e k r -> p e (k r)"),
                         fB.rearrange("e (p k) r -> p e (k r)", k=KT)).then_inc(d_bf, 16)
            sp.wait_ge(wq_laid, KT)
            for g in range(NG):
                sp.dma_start(Won[HD * g:HD * (g + 1)], wo.rearrange("(g h d) n -> g d h n", g=NG, h=PH)[g]).then_inc(d_o, 16)
            front_loads(1)
            load_xres(0)
            load_labels(0)
            with sp.Fori(0, G - 2) as g:
                front_loads(g + 2)
                back_loads(g + 1)
                store(g)
            back_loads(G - 1)
            store(G - 2)
            for t in range(TT):
                sp.wait_ge(fin_sb, TT * (G - 1) + t + 1)
                sp.dma_start(of[G - 1, t], xres[:, t, :]).then_inc(d_out, 16)
            sp.wait_ge(d_out, 16 * TT * G)

        @block.scalar
        def _(act):
            act.dma_start(K[:], consts).then_inc(d_K, 16)
            for c in range(KT):
                act.dma_start(Wn[:, c], cW[P * c:P * (c + 1)]).then_inc(d_W[c], 16)

            def copy(dst, src):
                return nc.scalar.copy(dst, src)

            def lay_adapters(g):
                act.wait_ge(d_slot, 16 * 2 * (SEQ * (g + 1) - POOL_SLOTS))
                if isinstance(g, int) and g == 0:
                    act.wait_ge(d_slot_pool, 16 * 2 * POOL_SLOTS)
                else:
                    act.wait_ge(h_ps, g)
                copy(A1[0][:].rearrange("p k s r -> p s k r"), A1n[:]).then_inc(a1_laid, 1)

            def lay_labels(g):
                act.wait_ge(d_a2, 16 * SEQ * (g + 1))
                if not (isinstance(g, int) and g == 0):
                    act.wait_ge(low_ps, TT * g)
                copy(A2[:].rearrange("p k s r -> p s k r"), A2n[:]).then_inc(a2_laid, 1)

            def x_cols(g):
                for h in range(2):
                    act.wait_ge(xT_ps, 2 * g + h + 1)
                    copy(xT[0][:, 2 * h:2 * h + 2].rearrange("p k t -> p (k t)"), FR[h][:]).then_inc(xT_sb, 1)

            def y_cols(g, h):
                act.wait_ge(y_ps, 2 * g + h + 1)
                for c in (2 * h, 2 * h + 1):
                    nc.scalar.activation(yT[:, c, :], FR[h][:, (c % 2) * TOK:(c % 2 + 1) * TOK], ACT.Identity,
                                         bias=bias[:, c:c + 1]).then_inc(y_sb, 1)

            def q_cols(g, h):
                act.wait_ge(q_ps, 2 * g + h + 1)
                copy(qh[:, 2 * h:2 * h + 2].rearrange("p k t -> p (k t)"), FR[h][:]).then_inc(q_sb, 1)

            def kv_cols(g):
                act.wait_ge(kv_ps, g + 1)
                copy(kT[:], SMALL[:, 0:TOK]).then_inc(kv_sb, 1)
                copy(v[0][:].rearrange("p t n -> p (t n)"), SMALL[:, TOK:2 * TOK]).then_inc(kv_sb, 1)

            def exp(g, j):
                act.wait_ge(shifted, PAIRS * g + j + 1)
                nc.scalar.activation(ex[:, j].rearrange("p a b -> p (a b)"), sm[:, j % 2].rearrange("p a b -> p (a b)"),
                                     ACT.Exp, scale=HD ** -0.5).then_inc(exped, 1)

            def pt_copy(g, j, src=PTB):
                act.wait_ge(pt_ps, PAIRS * g + j + 1)
                copy(PT[:, j % 2].rearrange("p a b c -> p (a b c)"), src[:]).then_inc(pt_sb, 1)

            def ctx_copy(g, j, src=CTX):
                act.wait_ge(ctx_ps, PAIRS * g + j + 1)
                copy(cT[0][:, :, 2 * j:2 * j + 2, :].rearrange("p h s t -> p s h t"),
                     src[:, 0:2 * P].rearrange("p (s h t) -> p s h t", s=2, h=PH)).then_inc(ctx_sb, 1)

            def x1_cols(g, t, tb=TB):
                act.wait_ge(x1T_ps, TT * g + t + 1)
                copy(x1T[:, t].rearrange("p k n -> p (k n)"), tb[t][:]).then_inc(x1T_sb, 1)

            def gate_exp(g, t=None):
                n, ts = (0, slice(0, TT)) if t is None else (t, slice(t, t + 1))
                act.wait_ge(g_step, STEPS * (g + n) + 4)
                nc.scalar.activation(le[:, ts].rearrange("p t e -> p (t e)"), lm[:, ts].rearrange("p t e -> p (t e)"),
                                     ACT.Exp).then_inc(g_exp, 1)

            def mgT_copy(g, t=None, tb=TB):
                for t in range(TT) if t is None else (t,):
                    act.wait_ge(mgT_ps, TT * g + t + 1)
                    copy(mgT[:, t], tb[t][:, 0:P]).then_inc(mgT_h, 1)

            def both(a, b, first=False):
                lay_adapters(a)
                x_cols(a)
                exp(b, 0)
                exp(b, 1)
                if not first:
                    gate_exp(b - 1)
                y_cols(a, 0)
                if not first:
                    mgT_copy(b - 1)
                y_cols(a, 1)
                pt_copy(b, 0)
                ctx_copy(b, 0)
                pt_copy(b, 1)
                exp(b, 2)
                q_cols(a, 0)
                ctx_copy(b, 1)
                exp(b, 3)
                pt_copy(b, 2)
                lay_labels(b)
                q_cols(a, 1)
                ctx_copy(b, 2)
                pt_copy(b, 3)
                kv_cols(a)
                ctx_copy(b, 3)
                x1_cols(b, 0)
                x1_cols(b, 1)

            act.wait_ge(zeroed, 1)
            nc.scalar.activation(gs[:], gr[:], ACT.Exp)
            act.dma_start(Wqn[:], wq.rearrange("(c p) n -> p c n", p=P)).then_inc(d_q, 16)
            x_cols(0)
            for k in range(KT):
                act.wait_ge(WT_ps, k + 1)
                copy(WT[0][:, k], bank[3 + k][:]).then_inc(WT_h, 1)
            lay_adapters(0)
            act.wait_ge(RAT_ps, 1)
            copy(RAT[:].rearrange("p c n -> p (c n)"), OUT[:, 0:KT * EW]).then_inc(RAT_sb, 1)
            act.wait_ge(d_b, 16)
            y_cols(0, 0)
            y_cols(0, 1)
            act.wait_ge(RT_ps, 1)
            copy(RT[:].rearrange("p c n -> p (c n)"), PTB[:, 0:KT * EW]).then_inc(RT_sb, 1)
            q_cols(0, 0)
            q_cols(0, 1)
            kv_cols(0)
            act.wait_ge(C4_ps, 1)
            copy(C4[:], OUT[:, 0:EW]).then_inc(C4_sb, 1)
            act.wait_ge(BT_ps, 1)
            nc.scalar.mul(BT[0][:].rearrange("q (p k) -> q k p", k=KT),
                          CTX[:].rearrange("q (k p) -> q k p", k=KT), 4.0).then_inc(BT_h, 1)
            act.wait_ge(d_o, 16 * NG)
            for h in range(PH):
                copy(Wo[0][:, h], Won[:, h]).then_inc(Wo_h, 1)
            both(1, 0, first=True)
            with act.Fori(1, G - 1) as g:
                both(g + 1, g)
            b = G - 1
            exp(b, 0)
            exp(b, 1)
            pt_copy(b, 0, FR[0])
            exp(b, 2)
            ctx_copy(b, 0, CTX)
            pt_copy(b, 1, FR[1])
            exp(b, 3)
            ctx_copy(b, 1, SMALL)
            lay_labels(b)
            pt_copy(b, 2, FR[0])
            gate_exp(b - 1)
            ctx_copy(b, 2, CTX)
            pt_copy(b, 3, FR[1])
            ctx_copy(b, 3, SMALL)
            mgT_copy(b - 1)
            x1_cols(b, 0, LB)
            x1_cols(b, 1, LB)
            gate_exp(b, 0)
            mgT_copy(b, 0, LB)
            gate_exp(b, 1)
            mgT_copy(b, 1, LB)

        @block.gpsimd
        def _(pool):
            def adapters_rest(g):
                pool.wait_ge(a1_laid, g + 1)
                if not (isinstance(g, int) and g == 0):
                    pool.wait_ge(h_ps, g)
                nc.gpsimd.tensor_tensor(A1[1][:].rearrange("p k s r -> p s k r"), A1n[:],
                                        A1[0][:].bitcast(F32).rearrange("p k s r -> p s k r"), ALU.subtract).then_inc(A1_l, 1)

            def norm(g, j):
                pool.wait_ge(recip, PAIRS * g + j + 1)
                nc.gpsimd.tensor_tensor(ex[:, j], ex[:, j],
                                        ri[:, j, :, None].broadcast_to((P, 2 * NG, T)), ALU.mult).then_inc(normed, 1)

            def shift(g, j):
                pool.wait_ge(maxed, PAIRS * g + j + 1)
                nc.gpsimd.tensor_tensor(sm[:, j % 2], sm[:, j % 2], mx[:, j, :, None].broadcast_to((P, 2 * NG, T)),
                                        ALU.subtract).then_inc(shifted, 1)

            def k_times_cos(g):
                pool.wait_ge(kv_sb, 2 * g + 1)
                nc.gpsimd.tensor_tensor(qkc[:, PH].rearrange("p (s t) -> p s t", t=T), kT[:].rearrange("p (s t) -> p s t", t=T),
                                        CS[:, 0, None, :].broadcast_to((P, SEQ, T)), ALU.mult).then_inc(k_cos, 1)

            def k_sum(g):
                pool.wait_ge(k_sin, g + 1)
                pool.wait_ge(k_cos, g + 1)
                nc.gpsimd.tensor_tensor(kr[:], qkc[:, PH], qks[:, PH], ALU.add).then_inc(k_rope, 1)

            def q_sum(g, h):
                pool.wait_ge(q_sin, 2 * g + h + 1)
                pool.wait_ge(q_cos, 2 * g + h + 1)
                s = slice(2 * h, 2 * h + 2)
                nc.gpsimd.tensor_tensor(qr[:, :, s, :].rearrange("p s h t -> p h s t"),
                                        qkc[:, s].rearrange("p h (s t) -> p h s t", t=T),
                                        qks[:, s].rearrange("p h (s t) -> p h s t", t=T), ALU.add).then_inc(q_rope, 1)

            def k_blocks(g, j):
                if j == 0:
                    pool.wait_ge(k_rope, g + 1)
                for s in (2 * j, 2 * j + 1):
                    i = nc.gpsimd.tensor_tensor(Kbd[:, s], kr[:, None, T * s:T * (s + 1)].broadcast_to((P, NG, T)),
                                                K[:, C_KG:C_KG + NG, None].broadcast_to((P, NG, T)), ALU.mult)
                i.then_inc(kbd_sb, 1)

            def rope(g):
                k_sum(g)
                k_blocks(g, 0)
                q_sum(g, 0)
                q_sum(g, 1)
                for j in range(1, PAIRS):
                    k_blocks(g, j)

            pool.wait_ge(d_ids, 32)
            load_slots(pool, 0, range(POOL_SLOTS), d_slot_pool)
            adapters_rest(0)
            pool.wait_ge(CS_sb, 1)
            k_times_cos(0)
            rope(0)
            with pool.Fori(0, G - 1) as g:
                adapters_rest(g + 1)
                norm(g, 0)
                norm(g, 1)
                norm(g, 2)
                norm(g, 3)
                k_times_cos(g + 1)
                rope(g + 1)
            b = G - 1
            shift(b, 1)
            norm(b, 0)
            shift(b, 2)
            norm(b, 1)
            shift(b, 3)
            norm(b, 2)
            norm(b, 3)

        @block.vector
        def _(dve):
            V = nc.vector

            def x_rest(g):
                for h in range(2):
                    dve.wait_ge(xT_sb, 2 * g + h + 1)
                    V.tensor_tensor(xT[1][:, 2 * h:2 * h + 2].rearrange("p k t -> p (k t)"), FR[h][:],
                                    xT[0][:, 2 * h:2 * h + 2].bitcast(F32).rearrange("p k t -> p (k t)"),
                                    ALU.subtract).then_inc(xT_l, 1)

            def y_split(g, h):
                for c in (2 * h, 2 * h + 1):
                    dve.wait_ge(y_sb, KT * g + c + 1)
                    V.tensor_copy(yS[0][:, c], yT[:, c]).then_inc(yT_h, 1)
                    dve.wait_ge(yT_h, KT * g + c + 1)
                    V.tensor_tensor(yS[1][:, c], yT[:, c], yS[0][:, c].bitcast(F32), ALU.subtract).then_inc(yT_l, 1)

            def ctx_rest(g, j, src=CTX):
                dve.wait_ge(ctx_sb, PAIRS * g + j + 1)
                V.tensor_tensor(cT[1][:, :, 2 * j:2 * j + 2, :].rearrange("p h s t -> p s h t"),
                                src[:, 0:2 * P].rearrange("p (s h t) -> p s h t", s=2, h=PH),
                                cT[0][:, :, 2 * j:2 * j + 2, :].bitcast(F32).rearrange("p h s t -> p s h t"),
                                ALU.subtract).then_inc(cT_l, 1)

            def adapter_mask(g):
                dve.wait_ge(h_ps, g + 1)
                V.tensor_tensor(hT[:].rearrange("p (s t) -> p s t", t=T), SMALL[:, 0:TOK].rearrange("p (s t) -> p s t", t=T),
                                K[:, C_SLOT:C_SLOT + SEQ, None].broadcast_to((P, SEQ, T)), ALU.mult).then_inc(h_sb, 1)

            def mask_max(g, j):
                dve.wait_ge(sc_ps, PAIRS * g + j + 1)
                V.tensor_tensor(sm[:, j % 2], SC[j % 2][:].rearrange("p (a s) -> p a s", s=T),
                                K[:, None, C_CAUSAL:C_CAUSAL + T].broadcast_to((P, 2 * NG, T)), ALU.add).then_inc(masked, 1)
                dve.wait_ge(masked, PAIRS * g + j + 1)
                V.tensor_reduce(mx[:, j], sm[:, j % 2], AX.X, ALU.max).then_inc(maxed, 1)

            def shift(g, j):
                mask_max(g, j)
                dve.wait_ge(maxed, PAIRS * g + j + 1)
                V.tensor_tensor(sm[:, j % 2], sm[:, j % 2], mx[:, j, :, None].broadcast_to((P, 2 * NG, T)),
                                ALU.subtract).then_inc(shifted, 1)

            def sums(g, j):
                dve.wait_ge(exped, PAIRS * g + j + 1)
                V.tensor_reduce(su[:, j], ex[:, j], AX.X, ALU.add).then_inc(summed, 1)
                dve.wait_ge(summed, PAIRS * g + j + 1)
                V.reciprocal(ri[:, j], su[:, j]).then_inc(recip, 1)

            def times_sin(dst, src, n):
                return V.tensor_tensor(dst, src, CS[:, 1, None, :].broadcast_to((P, n, T)), ALU.mult)

            def q_split(g, h):
                s = slice(2 * h, 2 * h + 2)
                dve.wait_ge(q_sb, 2 * g + h + 1)
                if not (isinstance(g, int) and g == 0):
                    dve.wait_ge(q_rope, 2 * g)
                V.tensor_tensor(ql[:, s].rearrange("p h t -> p (h t)"), FR[h][:],
                                qh[:, s].bitcast(F32).rearrange("p h t -> p (h t)"), ALU.subtract).then_inc(q_l, 1)
                V.tensor_tensor(qkc[:, s].rearrange("p h (s t) -> p (h s) t", t=T), FR[h][:].rearrange("p (a t) -> p a t", t=T),
                                CS[:, 0, None, :].broadcast_to((P, 2 * SEQ, T)), ALU.mult).then_inc(q_cos, 1)

            def k_times_sin(g):
                dve.wait_ge(rotk_ps, g + 1)
                times_sin(qks[:, PH].rearrange("p (s t) -> p s t", t=T),
                          SMALL[:, 0:TOK].rearrange("p (s t) -> p s t", t=T), SEQ).then_inc(k_sin, 1)

            def q_times_sin(g, h):
                dve.wait_ge(rotq_ps, 2 * g + h + 1)
                times_sin(qks[:, 2 * h:2 * h + 2].rearrange("p h (s t) -> p (h s) t", t=T),
                          FR[h][:].rearrange("p (a t) -> p a t", t=T), 2 * SEQ).then_inc(q_sin, 1)

            def v_rest(g):
                dve.wait_ge(kv_sb, 2 * g + 2)
                V.tensor_tensor(v[1][:].rearrange("p t n -> p (t n)"), SMALL[:, TOK:2 * TOK],
                                v[0][:].bitcast(F32).rearrange("p t n -> p (t n)"), ALU.subtract).then_inc(v_l, 1)

            def v_blocks(g, u):
                dve.wait_ge(vr_ps, 2 * g + u + 1)
                for half in range(2):
                    V.tensor_tensor(Vbd[:, half].rearrange("p (t s) (g d) -> p t s g d", t=TT, g=NG)[:, :, 2 * u:2 * u + 2]
                                    .rearrange("p t s g d -> p t (s g) d"),
                                    SMALL[:].rearrange("p (t m d) -> p t m d", t=TT, d=HD),
                                    K[:, None, C_VG + 2 * NG * half:C_VG + 2 * NG * (half + 1), None].broadcast_to((P, TT, 2 * NG, HD)),
                                    ALU.mult).then_inc(vbd_sb, 1)

            def residual(g, t, tb=TB, dst=None):
                dve.wait_ge(wo_ps, TT * g + t + 1)
                dve.wait_ge(d_xres, 16 * (TT * g + TT))
                if not (isinstance(g, int) and g in (0, G - 1)):
                    dve.wait_ge(d_out, 16 * TT * g)
                V.tensor_tensor((dst or x1)[:, t], tb[t][:], xres[:, t], ALU.add).then_inc(x1_sb, 1)

            def label_mask(g, t, tb=TB):
                dve.wait_ge(low_ps, TT * g + t + 1)
                V.tensor_tensor(lT[:, t].rearrange("p (s t) -> p s t", t=T), tb[t][:, 0:P].rearrange("p (s t) -> p s t", t=T),
                                K[:, C_LABEL:C_LABEL + 4, None].broadcast_to((P, 4, T)), ALU.mult).then_inc(low_sb, 1)

            def gates(g, one=None, tb=TB):
                tiles = range(TT) if one is None else (one,)
                n, ts, nt = (0, slice(0, TT), TT) if one is None else (one, slice(one, one + 1), 1)

                def step(ins):
                    ins.then_inc(g_step, 1)

                def after(i):
                    dve.wait_ge(g_step, STEPS * (g + n) + i)

                for t in tiles:
                    dve.wait_ge(mid_ps, TT * g + t + 1)
                    V.tensor_copy(mid[:, t], tb[t][:, 0:EW]).then_inc(mid_sb, 1)
                dve.wait_ge(mid_sb, TT * g + tiles[-1] + 1)
                lg = mid[:, ts, E * R:EW]
                of_j, of_e = lg[:, :, None, :].broadcast_to((P, nt, E, E)), lg[:, :, :, None].broadcast_to((P, nt, E, E))
                step(V.tensor_reduce(m1[:, ts], lg, AX.X, ALU.max))
                step(V.tensor_tensor(above[:, ts, :, 0], of_j, of_e, ALU.is_ge))
                step(V.tensor_tensor(above[:, ts, :, 1], of_j, of_e, ALU.is_gt))
                after(1)
                step(V.tensor_tensor(lm[:, ts], lg, m1[:, ts, None].broadcast_to((P, nt, E)), ALU.subtract))
                after(3)
                step(V.tensor_tensor(above[:, ts], above[:, ts], K[:, None, C_TRI:C_TRI + 2 * E * E].rearrange(
                    "p a (e c j) -> p a e c j", e=E, c=2).broadcast_to((P, nt, E, 2, E)), ALU.mult))
                after(5)
                step(V.tensor_reduce(rk[:, ts], above[:, ts].rearrange("p t e c j -> p t e (c j)"), AX.X, ALU.add))
                after(6)
                dve.wait_ge(g_exp, g + n + 1)
                step(V.scalar_tensor_tensor(out=gw[:, ts], in0=rk[:, ts], scalar=1.5, in1=le[:, ts],
                                            op0=ALU.is_lt, op1=ALU.mult))
                after(7)
                step(V.tensor_reduce(gs[:, ts], gw[:, ts], AX.X, ALU.add))
                after(8)
                step(V.reciprocal(gr[:, ts], gs[:, ts]))
                after(9)
                for t in tiles:
                    for i in range(2):
                        V.scalar_tensor_tensor(out=mg[:, t, i].rearrange("p (e r) -> p e r", e=E),
                                               in0=mid[:, t, 0:E * R].rearrange("p (e r) -> p e r", e=E), scalar=gr[:, t:t + 1],
                                               in1=gw[:, t, :, None].broadcast_to((P, E, R)), op0=ALU.mult,
                                               op1=ALU.mult).then_inc(g_mid, 1)

            def mgT_rest(g, t=None, tb=TB):
                for t in range(TT) if t is None else (t,):
                    dve.wait_ge(mgT_h, TT * g + t + 1)
                    V.tensor_tensor(mgT[E * R:P, t], tb[t][E * R:P, 0:P], mgT[E * R:P, t].bitcast(F32),
                                    ALU.subtract).then_inc(mgT_l, 1)

            def finish(g, order=(1, 0), tb=TB, dst=None):
                for n, t in enumerate(order):
                    dve.wait_ge(dl_ps, TT * g + n + 1)
                    V.tensor_tensor((dst or x1)[:, t], tb[t][:], (dst or x1)[:, t], ALU.add).then_inc(fin_sb, 1)

            def both(a, b, first=False):
                x_rest(a)
                if first:
                    shift(b, 0)
                shift(b, 1)
                sums(b, 0)
                adapter_mask(a)
                if not first:
                    gates(b - 1)
                y_split(a, 0)
                sums(b, 1)
                if not first:
                    mgT_rest(b - 1)
                    finish(b - 1)
                y_split(a, 1)
                shift(b, 2)
                ctx_rest(b, 0)
                sums(b, 2)
                shift(b, 3)
                ctx_rest(b, 1)
                sums(b, 3)
                q_split(a, 0)
                if first:
                    for h in range(PH):
                        dve.wait_ge(Wo_h, h + 1)
                        V.tensor_tensor(Wo[1][:, h], Won[:, h], Wo[0][:, h].bitcast(F32), ALU.subtract).then_inc(Wo_l, 1)
                ctx_rest(b, 2)
                q_split(a, 1)
                ctx_rest(b, 3)
                v_rest(a)
                k_times_sin(a)
                residual(b, 0)
                q_times_sin(a, 0)
                q_times_sin(a, 1)
                residual(b, 1)
                v_blocks(a, 0)
                label_mask(b, 0)
                v_blocks(a, 1)
                label_mask(b, 1)
                shift(a, 0)

            V.memset(gr[:], 0.0).then_inc(zeroed, 1)
            x_rest(0)
            for k in range(KT):
                dve.wait_ge(WT_h, k + 1)
                V.tensor_tensor(WT[1][:, k], bank[3 + k][:], WT[0][:, k].bitcast(F32), ALU.subtract).then_inc(WT_l, 1)
            dve.wait_ge(d_K, 16)
            V.tensor_copy(spread[:], ident.rearrange("p (s t) -> p s t", s=4)[:, :, None, :].broadcast_to((P, 4, 4, T))).then_inc(exact_laid, 1)
            V.tensor_copy(rot2[:], rot).then_inc(exact_laid, 1)
            dve.wait_ge(d_q, 16)
            for c in range(KT):
                wide = Wqn[:, c].rearrange("p (g h d) -> p h g d", g=NG, h=PH)
                V.tensor_copy(Wq[0][:, c].rearrange("p h (g d) -> p h g d", g=NG), wide).then_inc(Wq_h, 1)
                dve.wait_ge(Wq_h, c + 1)
                V.tensor_tensor(Wq[1][:, c].rearrange("p h (g d) -> p h g d", g=NG), wide,
                                Wq[0][:, c].bitcast(F32).rearrange("p h (g d) -> p h g d", g=NG), ALU.subtract).then_inc(wq_laid, 1)
            adapter_mask(0)
            dve.wait_ge(d_cs, 32)
            V.tensor_copy(cs8[:], cs[:, :, None, :].broadcast_to((T, 2, NG, HD))).then_inc(cs_laid, 1)
            y_split(0, 0)
            y_split(0, 1)
            dve.wait_ge(CS_ps, 1)
            V.tensor_copy(CS[:].rearrange("p a t -> p (a t)"), bank[3][:, 0:2 * T]).then_inc(CS_sb, 1)
            dve.wait_ge(d_k, 16)
            V.tensor_copy(Wk[0][:], Wkn[:]).then_inc(Wk_h, 1)
            dve.wait_ge(Wk_h, 1)
            V.tensor_tensor(Wk[1][:], Wkn[:], Wk[0][:].bitcast(F32), ALU.subtract).then_inc(Wk_l, 1)
            dve.wait_ge(d_bw, 16)
            V.tensor_copy(Bw4, Bw[:, :, None, :].broadcast_to((P, KT, 4, R2))).then_inc(bw_laid, 1)
            dve.wait_ge(d_bf, 16)
            for i in range(2):
                V.tensor_copy(Bk[:, :, i].rearrange("p k (e r) -> p k e r", e=E), Bf.rearrange("p e k r -> p k e r")).then_inc(bf_laid, 1)
            q_split(0, 0)
            q_split(0, 1)
            v_rest(0)
            k_times_sin(0)
            q_times_sin(0, 0)
            q_times_sin(0, 1)
            v_blocks(0, 0)
            v_blocks(0, 1)
            dve.wait_ge(BT_h, 1)
            V.scalar_tensor_tensor(out=BT[1][:].rearrange("q (p k) -> q k p", k=KT), in0=CTX[0:E * R].rearrange("q (k p) -> q k p", k=KT),
                                   scalar=4.0, in1=BT[0][0:E * R].bitcast(F32).rearrange("q (p k) -> q k p", k=KT),
                                   op0=ALU.mult, op1=ALU.subtract).then_inc(BT_l, 1)
            both(1, 0, first=True)
            with dve.Fori(1, G - 1) as g:
                both(g + 1, g)
            b = G - 1
            mask_max(b, 1)
            sums(b, 0)
            mask_max(b, 2)
            sums(b, 1)
            mask_max(b, 3)
            sums(b, 2)
            ctx_rest(b, 0, CTX)
            sums(b, 3)
            ctx_rest(b, 1, SMALL)
            gates(b - 1)
            ctx_rest(b, 2, CTX)
            residual(b, 0, LB, xres)
            ctx_rest(b, 3, SMALL)
            mgT_rest(b - 1)
            finish(b - 1)
            label_mask(b, 0, LB)
            residual(b, 1, LB, xres)
            gates(b, 0, LB)
            label_mask(b, 1, LB)
            mgT_rest(b, 0, LB)
            gates(b, 1, LB)
            mgT_rest(b, 1, LB)
            finish(b, (0, 1), LB, xres)

        @block.tensor
        def _(pe):
            def mm(dst, lhsT, rhs, start, stop):
                return nc.tensor.matmul(dst, lhsT, rhs, start=start, stop=stop)

            def mm3(dst, lhsT, rhs, start, stop):
                mm(dst, lhsT[0], rhs[0], start, False)
                mm(dst, lhsT[0], rhs[1], False, False)
                return mm(dst, lhsT[1], rhs[0], False, stop)

            def tr(dst, src, n=P):
                return nc.tensor.transpose(dst, src, ident[0:n, 0:n])

            def x_transposes(g):
                pe.wait_ge(d_x, 16 * (TT * g + TT))
                for h in range(2):
                    for k in (2 * h, 2 * h + 1):
                        for t in range(TT):
                            c = (k % 2) * TOK + t * P
                            i = tr(FR[h][:, c:c + P], xin[:, t, k:D:KT])
                    i.then_inc(xT_ps, 1)

            def adapter_in(g):
                pe.wait_ge(A1_l, g + 1)
                for k in range(KT):
                    i = mm3(SMALL[:, 0:TOK], [w[:, k].rearrange("p s r -> p (s r)") for w in A1],
                            [z[:, k] for z in xT], k == 0, k == KT - 1)
                i.then_inc(h_ps, 1)

            def y_base(g, h):
                for c in (2 * h, 2 * h + 1):
                    dst = FR[h][:, (c % 2) * TOK:(c % 2 + 1) * TOK]
                    for k in range(KT):
                        w, z = [w[:, k, P * c:P * (c + 1)] for w in WT], [z[:, k] for z in xT]
                        for n, (u, r) in enumerate(((0, 0), (0, 1), (1, 0))):
                            if isinstance(g, int) and g == 0 and c == 0 and n == 0:
                                pe.wait_ge(WT_l, k + 1)
                            nc.tensor.matmul(dst, w[u], z[r], start=(c % 2 == 0 and k == 0 and n == 0), stop=False,
                                             skip_group_check=True)

            def y_adapter(g, h):
                if h == 0:
                    pe.wait_ge(h_sb, g + 1)
                for c in (2 * h, 2 * h + 1):
                    dst = FR[h][:, (c % 2) * TOK:(c % 2 + 1) * TOK]
                    i = nc.tensor.matmul(dst, B1[:, P * c:P * (c + 1)], hT[:], start=False, stop=True, skip_group_check=True)
                i.then_inc(y_ps, 1)

            def y_tiles(g, h):
                y_base(g, h)
                y_adapter(g, h)

            def q_tiles(g, h):
                if h == 0:
                    pe.wait_ge(yT_l, KT * (g + 1))
                for q in (2 * h, 2 * h + 1):
                    dst = FR[h][:, (q % 2) * TOK:(q % 2 + 1) * TOK]
                    for c in range(KT):
                        i = mm3(dst, [w[:, c, q] for w in Wq], [z[:, c] for z in yS], c == 0, c == KT - 1)
                i.then_inc(q_ps, 1)

            def kv_tiles(g):
                for c in range(KT):
                    mm3(SMALL[:, 0:TOK], [w[:, c] for w in Wk], [z[:, c] for z in yS], c == 0, c == KT - 1)
                for t in range(TT):
                    for c in range(KT):
                        i = mm(SMALL[:, TOK + P * t:TOK + P * (t + 1)], yT[:, c, P * t:P * (t + 1)], Wv[:, c],
                               c == 0, c == KT - 1)
                i.then_inc(kv_ps, 1)

            def rotate_k(g):
                pe.wait_ge(kv_sb, 2 * g + 1)
                pe.wait_ge(v_l, g + 1)
                mm(SMALL[:, 0:TOK], rot, kT[:], True, True).then_inc(rotk_ps, 1)

            def rotate_q(g):
                for h in range(2):
                    pe.wait_ge(q_l, 2 * g + h + 1)
                    pe.wait_ge(q_cos, 2 * g + h + 1)
                    mm(FR[h][:], rot2[:], qh[:, 2 * h:2 * h + 2].rearrange("p h t -> p (h t)"), True, False)
                    mm(FR[h][:], rot2[:], ql[:, 2 * h:2 * h + 2].rearrange("p h t -> p (h t)"), False, True).then_inc(rotq_ps, 1)

            def v_spread(g, u):
                if u == 0:
                    pe.wait_ge(k_sin, g + 1)
                else:
                    pe.wait_ge(vbd_sb, 4 * g + 2)
                for s in range(2):
                    dst = SMALL[:].rearrange("p (t s n) -> p s t n", t=TT, s=2)[:, s]
                    w = spread[:, 2 * u + s].rearrange("p a t -> p (a t)")
                    mm(dst, w, v[0][:], True, False)
                    i = mm(dst, w, v[1][:], False, True)
                i.then_inc(vr_ps, 1)

            def scores(g, j):
                if j < 2:
                    pe.wait_ge(q_rope, 2 * g + 2)
                    if not (isinstance(g, int) and g == 0):
                        pe.wait_ge(masked, PAIRS * g - 2 + j + 1)
                else:
                    pe.wait_ge(masked, PAIRS * g + j - 1)
                pe.wait_ge(kbd_sb, PAIRS * g + j + 1)
                for s in range(2):
                    i = mm(SC[j % 2][:, 2 * P * s:2 * P * (s + 1)], qr[:, 2 * j + s].rearrange("p h t -> p (h t)"),
                           Kbd[:, 2 * j + s].rearrange("p g t -> p (g t)"), True, True)
                i.then_inc(sc_ps, 1)

            def p_transposes(g, j, dst=PTB, banks=1):
                pe.wait_ge(normed, PAIRS * g + j + 1)
                if j >= banks:
                    pe.wait_ge(pt_sb, PAIRS * g + j - banks + 1)
                for s in range(2):
                    for half in range(2):
                        c = (2 * s + half) * P
                        i = tr(dst[:, c:c + P], ex[:, j].rearrange("p a t -> p (a t)")[:, c:c + P])
                i.then_inc(pt_ps, 1)

            def context(g, j, dst=CTX, banks=1):
                pe.wait_ge(pt_sb, PAIRS * g + j + 1)
                if j == 0:
                    pe.wait_ge(vbd_sb, 4 * (g + 1))
                if j >= banks:
                    pe.wait_ge(cT_l, PAIRS * g + j - banks + 1)
                for s in range(2):
                    for half in range(2):
                        i = mm(dst[:, P * s:P * (s + 1)], Vbd[:, half, 2 * j + s], PT[:, j % 2, s, half], half == 0, half == 1)
                i.then_inc(ctx_ps, 1)

            def project(g, t, tb=TB):
                pe.wait_ge(cT_l, PAIRS * g + 2 * (t + 1))
                if isinstance(g, int) and g == 0 and t == 0:
                    pe.wait_ge(Wo_l, PH)
                for h in range(PH):
                    i = mm3(tb[t][:], [c[:, h, 4 * t:4 * t + 4].rearrange("p s t -> p (s t)") for c in cT],
                            [w[:, h] for w in Wo], h == 0, h == PH - 1)
                i.then_inc(wo_ps, 1)

            def x1_transposes(g, t, tb=TB, src=None):
                pe.wait_ge(x1_sb, TT * g + t + 1)
                for k in range(KT):
                    i = tr(tb[t][:, P * k:P * (k + 1)], (src or x1)[:, t, k:D:KT])
                i.then_inc(x1T_ps, 1)

            def label_in(g, t, tb=TB):
                pe.wait_ge(x1T_sb, TT * g + t + 1)
                pe.wait_ge(a2_laid, g + 1)
                for k in range(KT):
                    i = mm(tb[t][:, 0:P], A2[:, k, 4 * t:4 * t + 4].rearrange("p s r -> p (s r)"), x1T[:, t, k], k == 0, k == KT - 1)
                i.then_inc(low_ps, 1)

            def mid_logits(g, t, tb=TB):
                pe.wait_ge(low_sb, TT * g + t + 1)
                for k in range(KT):
                    mm(tb[t][:, 0:EW], x1T[:, t, k], RT[:, k], k == 0, False)
                mm(tb[t][:, 0:EW], lT[:, t], C4[:], False, True).then_inc(mid_ps, 1)

            def mid_transpose(g, t, tb=TB):
                pe.wait_ge(g_mid, 2 * (TT * g + t + 1))
                tr(tb[t][:, 0:P], mg[:, t].rearrange("p a n -> p (a n)")).then_inc(mgT_ps, 1)

            def delta(g, t, copied=TT, tb=TB):
                pe.wait_ge(mgT_l, TT * g + copied)
                mm(tb[t][:], mgT[:, t], BT[0][:], True, False)
                mm(tb[t][:], mgT[0:E * R, t], BT[1][:], False, True).then_inc(dl_ps, 1)

            def both(a, b, first=False):
                x_transposes(a)
                if first:
                    scores(b, 0)
                    scores(b, 1)
                else:
                    mid_logits(b - 1, 0)
                    mid_logits(b - 1, 1)
                pe.wait_ge(xT_l, 2 * a + 2)
                if first:
                    y_base(a, 0)
                    adapter_in(a)
                    y_base(a, 1)
                    y_adapter(a, 0)
                else:
                    adapter_in(a)
                    y_tiles(a, 0)
                    y_base(a, 1)
                    mid_transpose(b - 1, 0)
                    mid_transpose(b - 1, 1)
                y_adapter(a, 1)
                if not first:
                    delta(b - 1, 1)
                    delta(b - 1, 0)
                scores(b, 2)
                if not first:
                    pe.wait_ge(fin_sb, TT * (b - 1) + 1)
                p_transposes(b, 0)
                scores(b, 3)
                if first:
                    pe.wait_ge(BT_l, 1)
                context(b, 0)
                p_transposes(b, 1)
                q_tiles(a, 0)
                context(b, 1)
                p_transposes(b, 2)
                q_tiles(a, 1)
                context(b, 2)
                p_transposes(b, 3)
                kv_tiles(a)
                context(b, 3)
                if not first:
                    pe.wait_ge(fin_sb, TT * b)
                project(b, 0)
                rotate_k(a)
                rotate_q(a)
                project(b, 1)
                x1_transposes(b, 0)
                v_spread(a, 0)
                x1_transposes(b, 1)
                label_in(b, 0)
                scores(a, 0)
                v_spread(a, 1)
                label_in(b, 1)
                scores(a, 1)

            pe.wait_ge(d_K, 16)
            x_transposes(0)
            for c in range(KT):
                pe.wait_ge(d_W[c], 16)
                for k in range(KT):
                    i = tr(bank[3 + k][:, P * c:P * (c + 1)], Wn[:, c, k:D:KT])
                    if c == KT - 1:
                        i.then_inc(WT_ps, 1)
            pe.wait_ge(xT_l, 2)
            y_base(0, 0)
            y_base(0, 1)
            pe.wait_ge(d_ra, 32)
            for c in range(KT):
                i = tr(OUT[:, EW * c:EW * (c + 1)], RA[:, P * c:P * (c + 1)], EW)
            i.then_inc(RAT_ps, 1)
            adapter_in(0)
            y_adapter(0, 0)
            y_adapter(0, 1)
            pe.wait_ge(cs_laid, 1)
            for a in range(2):
                i = mm(bank[3][:, T * a:T * (a + 1)], cs8[:, a].rearrange("t g d -> t (g d)"), ident[0:T, 0:T], True, True)
            i.then_inc(CS_ps, 1)
            pe.wait_ge(RAT_sb, 1)
            pe.wait_ge(d_w2, 16)
            for k in range(KT):
                for c in range(KT):
                    i = mm(PTB[:, EW * k:EW * (k + 1)], W2[:, c, k:D:KT], RAT[:, c], c == 0, c == KT - 1)
            i.then_inc(RT_ps, 1)
            pe.wait_ge(wq_laid, KT)
            q_tiles(0, 0)
            q_tiles(0, 1)
            pe.wait_ge(Wk_l, 1)
            pe.wait_ge(d_v, 16)
            kv_tiles(0)
            pe.wait_ge(bw_laid, 1)
            for c in range(KT):
                i = mm(OUT[:, 0:EW], Bw4[:, c].rearrange("p a r -> p (a r)"), RAT[:, c], c == 0, c == KT - 1)
            i.then_inc(C4_ps, 1)
            pe.wait_ge(exact_laid, 2)
            rotate_k(0)
            rotate_q(0)
            v_spread(0, 0)
            pe.wait_ge(bf_laid, 2)
            for c in range(KT):
                i = tr(CTX[:, P * c:P * (c + 1)], Bk[:, c].rearrange("p a n -> p (a n)"))
            i.then_inc(BT_ps, 1)
            v_spread(0, 1)
            pe.wait_ge(RT_sb, 1)
            pe.wait_ge(C4_sb, 1)
            both(1, 0, first=True)
            with pe.Fori(1, G - 1) as g:
                both(g + 1, g)
            b = G - 1
            scores(b, 2)
            mid_logits(b - 1, 0)
            mid_logits(b - 1, 1)
            scores(b, 3)
            p_transposes(b, 0, FR[0], 2)
            context(b, 0, CTX, 2)
            p_transposes(b, 1, FR[1], 2)
            context(b, 1, SMALL, 2)
            p_transposes(b, 2, FR[0], 2)
            project(b, 0, LB)
            context(b, 2, CTX, 2)
            p_transposes(b, 3, FR[1], 2)
            context(b, 3, SMALL, 2)
            mid_transpose(b - 1, 0)
            mid_transpose(b - 1, 1)
            x1_transposes(b, 0, LB, xres)
            delta(b - 1, 1)
            delta(b - 1, 0)
            label_in(b, 0, LB)
            project(b, 1, LB)
            mid_logits(b, 0, LB)
            x1_transposes(b, 1, LB, xres)
            label_in(b, 1, LB)
            mid_transpose(b, 0, LB)
            mid_logits(b, 1, LB)
            delta(b, 0, 1, LB)
            mid_transpose(b, 1, LB)
            delta(b, 1, TT, LB)


_INS = ["x", "itok_B_0_23", "itok_B_0_2", "L0_cond_W", "L0_cond_b", "L0_cond_lora_As", "L0_cond_lora_Bs",
        "L0_attn_Wq", "L0_attn_Wk", "L0_attn_Wv", "L0_attn_Wo", "L0_attn_cos", "L0_attn_sin",
        "L0_cond2_W", "L0_cond2_lora_A", "L0_cond2_lora_B_w", "L0_ffn_router_w", "L0_ffn_A", "L0_ffn_B"]


def kernel(**inputs):
    import concourse.bacc as bacc
    from concourse.bass_utils import run_bass_kernel_spmd

    nc = bacc.Bacc("TRN2", target_bir_lowering=False, num_devices=1)
    arrays, args = {}, []
    for name in _INS:
        a = np.ascontiguousarray(inputs[name])
        arrays[name] = a
        args.append(nc.dram_tensor(name, a.shape, mybir.dt.from_np(a.dtype), kind="ExternalInput").ap())
    arrays["constants"] = shape_constants()
    args.append(nc.dram_tensor("constants", (P, C_N), F32, kind="ExternalInput").ap())
    args.append(nc.dram_tensor("out", (B, T, D), F32, kind="ExternalOutput").ap())
    program(nc, *args)
    r = run_bass_kernel_spmd(nc, [arrays], core_ids=[0])
    return r.results[0]["out"]
```
